# Optimizing a Trainium2 kernel written in Bass

```python
import numpy as np
import jax
import jax.numpy as jnp

def _softmax(x, axis=-1):
    return jax.nn.softmax(x, axis=axis)

def _gelu(x):
    return jax.nn.gelu(x, approximate=True)

def _silu(x):
    return jax.nn.silu(x)

def _sigmoid(x):
    return jax.nn.sigmoid(x)

def _layernorm(x, axis=-1, eps=1e-05):
    m = jnp.mean(x, axis=axis, keepdims=True)
    v = jnp.var(x, axis=axis, keepdims=True)
    return (x - m) / jnp.sqrt(v + eps)

def _scatter_add(tgt, idx, src, axis=0):
    return tgt.at[idx].add(src)

def _segment_sum(src, seg, n):
    return jax.ops.segment_sum(src, seg, n)
kernel_name = 'mk_metaformer_d1_conv_nchw768_r4_2f63f2'

def setup_inputs(seed: int=0):
    np.random.seed(seed)
    _w = jnp.asarray

    def _rec_inputs():
        import jax
        import jax.numpy as jnp
        _gk = jax.random.key(seed)
        x = -0.0002221 + 1 * jax.random.normal(jax.random.fold_in(_gk, 1), (8, 192, 16, 16), jnp.float32)
        return x
    x = _rec_inputs()

    def _L0_conv_setup():
        import jax, jax.numpy as jnp
        import numpy as np
        K = 7
        PAD = K // 2
        EPS = 1e-12

        def _offsets():
            offs = []
            offs += [(i, i) for i in range(K)]
            offs += [(i, K // 2) for i in range(K)]
            offs += [(i, K - 1 - i) for i in range(K)]
            offs += [(K // 2, i) for i in range(K)]
            return offs
        key = jax.random.key(seed)
        k1, k2, k3 = jax.random.split(key, 3)
        B, C, H, W = (8, 192, 16, 16)
        OUT_C = 192
        feature = jax.random.normal(k1, (B, C, H, W), dtype=jnp.float32)
        conv_w = jax.random.normal(k2, (OUT_C, C + 4 * K), dtype=jnp.float32) * 0.02
        conv_b = jax.random.normal(k3, (OUT_C,), dtype=jnp.float32) * 0.02
        return {'feature': feature, 'conv_w': conv_w, 'conv_b': conv_b}
    _L0_conv_all = _L0_conv_setup()
    _L0_conv_in = {k: v for k, v in _L0_conv_all.items() if k in ('conv_w', 'conv_b')}
    del _L0_conv_all

    def _L0_ffn_setup():
        import jax, jax.numpy as jnp
        import numpy as np
        E = 8
        TOP_K = 2
        CAP_RATIO = 1.2
        key = jax.random.key(seed)
        k1, k2, k3, k4 = jax.random.split(key, 4)
        B, L, D, H = (2, 512, 192, 512)
        x = jax.random.normal(k1, (B, L, D), dtype=jnp.float32)
        Wg = jax.random.normal(k2, (D, E), dtype=jnp.float32) * 0.02
        W1 = jax.random.normal(k3, (E, D, 2 * H), dtype=jnp.float32) * 0.02
        W2 = jax.random.normal(k4, (E, H, D), dtype=jnp.float32) * 0.02
        return {'x': x, 'Wg': Wg, 'W1': W1, 'W2': W2}
    _L0_ffn_all = _L0_ffn_setup()
    _L0_ffn_in = {k: v for k, v in _L0_ffn_all.items() if k in ('Wg', 'W1', 'W2')}
    del _L0_ffn_all
    return {'x': x, 'L0_conv_conv_w': _L0_conv_in['conv_w'], 'L0_conv_conv_b': _L0_conv_in['conv_b'], 'L0_ffn_Wg': _L0_ffn_in['Wg'], 'L0_ffn_W1': _L0_ffn_in['W1'], 'L0_ffn_W2': _L0_ffn_in['W2']}

def reference(x, L0_conv_conv_w, L0_conv_conv_b, L0_ffn_Wg, L0_ffn_W1, L0_ffn_W2):
    import jax
    import jax.numpy as jnp

    def _L0_conv_ref(feature, conv_w, conv_b):
        import jax, jax.numpy as jnp
        import numpy as np
        K = 7
        PAD = K // 2
        EPS = 1e-12

        def _offsets():
            offs = []
            offs += [(i, i) for i in range(K)]
            offs += [(i, K // 2) for i in range(K)]
            offs += [(i, K - 1 - i) for i in range(K)]
            offs += [(K // 2, i) for i in range(K)]
            return offs
        b, c, h, w = feature.shape
        norm = jnp.sqrt(jnp.sum(feature * feature, axis=1, keepdims=True))
        feat_n = feature / jnp.maximum(norm, EPS)
        feat_pad = jnp.pad(feat_n, ((0, 0), (0, 0), (PAD, PAD), (PAD, PAD)))
        corr = jnp.stack([jnp.sum(feat_pad[:, :, r:h + r, cc:w + cc] * feat_n, axis=1) for r, cc in _offsets()], axis=1)
        x = jnp.concatenate([feature, corr], axis=1)
        out = jnp.einsum('bchw,oc->bohw', x, conv_w) + conv_b[None, :, None, None]
        return out

    def _L0_ffn_ref(x, Wg, W1, W2):
        import jax, jax.numpy as jnp
        import numpy as np
        E = 8
        TOP_K = 2
        CAP_RATIO = 1.2
        B, L, D = x.shape
        H = W2.shape[1]
        xf = x.reshape(-1, D)
        N = xf.shape[0]
        capacity = int(CAP_RATIO * N / E)
        logits = xf @ Wg
        scores, idx = jax.lax.top_k(logits, TOP_K)
        weights = jax.nn.softmax(scores, axis=-1)
        xpad = jnp.concatenate([xf, jnp.zeros((1, D), xf.dtype)], axis=0)
        wpad_zero = jnp.zeros((1,), weights.dtype)
        out = jnp.zeros((N, D), x.dtype)
        for k in range(TOP_K):
            ik = idx[:, k]
            onehot = ik[:, None] == jnp.arange(E)[None, :]
            pos = jnp.cumsum(onehot, axis=0) - 1
            posk = jnp.take_along_axis(pos, ik[:, None], axis=1)[:, 0]
            keep = posk < capacity
            buf = jnp.full((E, capacity), N, dtype=jnp.int32)
            buf = buf.at[ik, posk].set(jnp.arange(N, dtype=jnp.int32), mode='drop')
            xg = xpad[buf]
            h = jnp.einsum('ecd,edh->ech', xg, W1)
            act = h[..., :H] * jax.nn.silu(h[..., H:])
            ye = jnp.einsum('ech,ehd->ecd', act, W2)
            wk = jnp.where(keep, weights[:, k], 0.0)
            w_buf = jnp.concatenate([wk, wpad_zero])[buf]
            out = out.at[buf.reshape(-1)].add((w_buf[..., None] * ye).reshape(E * capacity, D), mode='drop')
        return out.reshape(B, L, D)

    def _gn(v, G=32, eps=1e-05):
        B_, C_, H_, W_ = v.shape
        g = v.reshape(B_, G, C_ // G, H_, W_)
        m = jnp.mean(g, axis=(2, 3, 4), keepdims=True)
        s = jnp.var(g, axis=(2, 3, 4), keepdims=True)
        return ((g - m) / jnp.sqrt(s + eps)).reshape(v.shape)

    def _ln_c(v, eps=1e-06):
        m = jnp.mean(v, axis=1, keepdims=True)
        s = jnp.var(v, axis=1, keepdims=True)
        return (v - m) / jnp.sqrt(s + eps)

    def _ln_t(v, eps=1e-05):
        m = jnp.mean(v, axis=-1, keepdims=True)
        s = jnp.var(v, axis=-1, keepdims=True)
        return (v - m) / jnp.sqrt(s + eps)

    def _to_tokens(v):
        B_, C_, H_, W_ = v.shape
        return v.reshape(B_, C_, H_ * W_).transpose(0, 2, 1)

    def _from_tokens(t, like):
        B_, C_, H_, W_ = like.shape
        return t.transpose(0, 2, 1).reshape(B_, C_, H_, W_)
    x = x + _L0_conv_ref(_ln_c(x), L0_conv_conv_w, L0_conv_conv_b)
    t = _to_tokens(x)
    t = t + _L0_ffn_ref(_ln_t(t), L0_ffn_Wg, L0_ffn_W1, L0_ffn_W2)
    x = _from_tokens(t, x)
    return x

_drawn_inputs = setup_inputs


def setup_inputs(seed=0):
    import zlib

    import numpy as np

    out = dict(_drawn_inputs(seed))
    spreads = {}
    factors = {'L0_conv_conv_b': 2.894, 'L0_ffn_Wg': 5.361, 'L0_ffn_W1': 4.639, 'L0_ffn_W2': 4.642}
    for name, (base, spread) in spreads.items():
        noise = np.random.default_rng([zlib.crc32(name.encode()), seed]).standard_normal(out[name].shape)
        drawn = base * np.exp(spread * noise) if base else spread * noise
        out[name] = jnp.asarray(drawn.astype(out[name].dtype))
    for name, factor in factors.items():
        out[name] = (out[name] * factor).astype(out[name].dtype)
    return out
```

```python
from contextlib import ExitStack

import numpy as np
import concourse.bass as bass
from concourse import mybir

F32 = mybir.dt.float32
F32R = mybir.dt.float32r
BF16 = mybir.dt.bfloat16
I32 = mybir.dt.int32
U32 = mybir.dt.uint32
ALU = mybir.AluOpType
ACT = mybir.ActivationFunctionType
AX_X = mybir.AxisListType.X

P = 128
IMAGES, C, SIDE = 8, 192, 16
PIXELS = SIDE * SIDE
TOKENS = IMAGES * PIXELS
CB = C - P
TILES = 4
GROUP = TILES * P
GROUPS = TOKENS // GROUP
K = 7
PAD = K // 2
NCORR = 4 * K
REACH = PAD * SIDE + PAD
SPAN = 2 * REACH + 1
WIN = P + 2 * REACH
SKEW = WIN + 1
E, TOPK, H = 8, 2, 512
CAP = int(1.2 * TOKENS / E)
SLOT_TILES = -(-TOPK * CAP // P)
SLOTS = SLOT_TILES * P
USED = TOPK * CAP
CHUNKS = [(0, (USED // 2 + 1) // 2 * 2), ((USED // 2 + 1) // 2 * 2, USED)]
CHUNK = CHUNKS[0][1]
ROW = C + 2
NH = H // P
MISS = float(1 << 20)
LOWEST = -3.0e38

C_IDENT = 0
C_UPPER = C_IDENT + P
C_REV = C_UPPER + P
C_MASK = C_REV + E
C_KOFF = C_MASK + TILES * NCORR
C_TOK = C_KOFF + TILES * TOPK
C_SIGN = C_TOK + GROUPS * TILES
C_SPARE = C_SIGN + SLOT_TILES
C_ALL = C_SPARE + SLOT_TILES


def constants():
    c = np.zeros((P, C_ALL), np.float32)
    p = np.arange(P)
    c[:, C_IDENT:C_IDENT + P] = np.eye(P)
    c[:, C_UPPER:C_UPPER + P] = p[:, None] < p[None, :]
    c[:, C_REV:C_REV + E] = E - np.arange(E)
    offsets = [(i, i) for i in range(K)] + [(i, PAD) for i in range(K)]
    offsets += [(i, K - 1 - i) for i in range(K)] + [(PAD, i) for i in range(K)]
    for t in range(TILES):
        pixel = (t * P + p) % PIXELS
        for n, (r, s) in enumerate(offsets):
            y, x = pixel // SIDE + r - PAD, pixel % SIDE + s - PAD
            c[:, C_MASK + t * NCORR + n] = (y >= 0) & (y < SIDE) & (x >= 0) & (x < SIDE)
        for k in range(TOPK):
            c[:, C_KOFF + t * TOPK + k] = E * SLOTS + k * CAP
    for t in range(GROUPS * TILES):
        c[:, C_TOK + t] = t * P + p
    for t in range(SLOT_TILES):
        c[:, C_SIGN + t] = np.where(t * P + p < CAP, -1.0, 1.0)
        c[:, C_SPARE + t] = TOKENS + t * P + p
    return c


class Count:

    def __init__(self, base):
        self.base, self.n = base, 0

    def up(self):
        self.n += 1
        return 1

    @property
    def now(self):
        return self.base + self.n


A_STEPS = 5
B_STEPS = 18


def metaformer_kernel(nc, x, conv_wt, wg, w1, w2, consts, out):
    gram_dram = nc.dram_tensor("gram_dram", [GROUPS, TILES, P * SKEW], F32, kind="Internal").ap()
    table = nc.dram_tensor("slot_table", [E * SLOTS, ROW], F32, kind="Internal").ap()

    with ExitStack() as ctx:
        def sb(name, shape, dt=F32):
            return ctx.enter_context(nc.sbuf_tensor(name, shape, dt))

        def sem(name):
            return ctx.enter_context(nc.semaphore(name))

        bank = [ctx.enter_context(nc.psum_tensor(f"bank{i}", [P, 512], F32)) for i in range(8)]

        cst = sb("cst", [P, C_ALL])
        ident = cst[:, C_IDENT:C_IDENT + P]
        rev = cst[:, C_REV:C_REV + E]
        mask = cst[:, C_MASK:C_KOFF].rearrange("p (t n) -> p t n", t=TILES)
        koff = cst[:, C_KOFF:C_TOK]
        sign = cst[:, C_SIGN:C_SPARE]
        spare = cst[:, C_SPARE:C_ALL]
        before = sb("before", [P, P], BF16)
        ones = sb("ones", [P, P], BF16)
        eps_c = sb("eps_c", [P, 1])
        eps_t = sb("eps_t", [P, 1])
        conv_a = sb("conv_a", [P, C])
        conv_b = sb("conv_b", [CB + NCORR + 1, C])
        wg_a = sb("wg_a", [P, E])
        wg_b = sb("wg_b", [CB, E])
        empty = sb("empty", [P, SLOT_TILES, ROW])

        xt = sb("xt", [P, GROUPS * TILES, C])
        f = sb("f", [P, TILES, C])
        fc = sb("fc", [P, TILES, CB + NCORR + 1])
        ft_a = sb("ft_a", [P, GROUP + 2 * REACH])
        ft_b = sb("ft_b", [CB, GROUP + 2 * REACH])
        ct = sb("ct", [CB + NCORR + 1, GROUP])
        gram = sb("gram", [P, TILES, WIN])
        near = sb("near", [P, TILES, SPAN])
        stat_a = sb("stat_a", [P, TILES, 6])
        mv_a = sb("mv_a", [P, TILES, 2])
        stat_b = sb("stat_b", [P, TILES, 6])
        mv_b = sb("mv_b", [P, TILES, 2])
        sd_a = sb("sd_a", [P, TILES])
        len_a = sb("len_a", [P, TILES])
        rstd_a = sb("rstd_a", [P, TILES])
        nrm_a = sb("nrm_a", [P, TILES])
        q_a = sb("q_a", [P, TILES])
        norm = sb("norm", [P, GROUPS * TILES])
        inv_norm = sb("inv_norm", [P, GROUPS * TILES])
        sd_b = sb("sd_b", [P, TILES])
        rstd_b = sb("rstd_b", [P, TILES])
        row = sb("row", [P, TILES, ROW])
        tt_a = sb("tt_a", [P, GROUP])
        tt_b = sb("tt_b", [CB, GROUP])
        lg = sb("lg", [P, TILES, E])
        lg2 = sb("lg2", [P, TILES, E])
        top = sb("top", [P, TILES, TOPK])
        is_top = sb("is_top", [P, TILES, E])
        ranked = sb("ranked", [P, TILES, E])
        pick = sb("pick", [P, TILES, TOPK])
        onehot = sb("onehot", [P, TILES, TOPK, E], BF16)
        seen = sb("seen", [P, TILES + 1, TOPK * E], BF16)
        place_e = sb("place_e", [P, TILES * TOPK, E])
        place = sb("place", [P, TILES * TOPK])
        miss = sb("miss", [P, TILES * TOPK])
        region = sb("region", [P, TILES * TOPK])
        slot_f = sb("slot_f", [P, TILES * TOPK])
        slot = sb("slot", [P, TILES * TOPK], U32)

        raw_a = [sb(f"raw_a{b}", [P, 2 * H]) for b in range(2)]
        raw_b = [sb(f"raw_b{b}", [P, 2 * H]) for b in range(2)]
        raw_2 = [sb(f"raw_2{b}", [P, NH * C]) for b in range(2)]
        hi_a = [sb(f"hi_a{b}", [P, 2 * H], F32R) for b in range(2)]
        hi_b = [sb(f"hi_b{b}", [P, 2 * H], F32R) for b in range(2)]
        hi_2 = [sb(f"hi_2{b}", [P, NH * C], F32R) for b in range(2)]
        lo_a = [sb(f"lo_a{b}", [P, 2 * H], F32R) for b in range(2)]
        lo_b = [sb(f"lo_b{b}", [P, 2 * H], F32R) for b in range(2)]
        lo_2 = [sb(f"lo_2{b}", [P, NH * C], F32R) for b in range(2)]
        rows = [sb(f"rows{b}", [P, SLOT_TILES, ROW + CB]) for b in range(2)]
        arg = sb("arg", [P, SLOT_TILES])
        th = sb("th", [P, SLOT_TILES])
        wt = [sb(f"wt{b}", [P, SLOT_TILES]) for b in range(2)]
        xh_a = sb("xh_a", [P, USED], F32R)
        xl_a = sb("xl_a", [P, USED], F32R)
        x_b = sb("x_b", [P, USED], F32R)
        sil = [sb(f"sil{b}", [P, CHUNK]) for b in range(2)]
        act = [sb(f"act{b}", [P, CHUNK]) for b in range(3)]
        ah = sb("ah", [P, NH, USED], F32R)
        al = sb("al", [P, NH, USED], F32R)
        y = sb("y", [P, SLOT_TILES, C])

        x_first = sem("x_first"); x_rest = sem("x_rest"); cst_in = sem("cst_in")
        w_in = [sem(f"w_in{b}") for b in range(2)]
        rows_in = [sem(f"rows_in{b}") for b in range(2)]
        cst_ready = sem("cst_ready"); passed = sem("passed")
        a_step = sem("a_step"); b_step = sem("b_step")
        var_a = sem("var_a"); sqrt_a = sem("sqrt_a"); f_ready = sem("f_ready"); f_q = sem("f_q")
        fc_copied = sem("fc_copied"); f_turned = sem("f_turned"); ft_ready = sem("ft_ready")
        gram_done = sem("gram_done"); gram_sb = sem("gram_sb")
        gram_out = sem("gram_out"); near_in = sem("near_in")
        corr_ready = sem("corr_ready"); c_turned = sem("c_turned"); ct_ready = sem("ct_ready")
        conv_done = sem("conv_done"); x1_ready = sem("x1_ready"); x1_out = sem("x1_out")
        var_b = sem("var_b"); sqrt_b = sem("sqrt_b"); tn_ready = sem("tn_ready")
        t_turned = sem("t_turned"); tt_ready = sem("tt_ready"); logits_done = sem("logits_done")
        choice_ready = sem("choice_ready"); place_done = sem("place_done")
        slot_ready = sem("slot_ready"); table_out = sem("table_out")
        w_hi = sem("w_hi"); w_lo = sem("w_lo"); rows_turned = sem("rows_turned")
        x_hi = sem("x_hi"); x_lo = sem("x_lo"); h_done = sem("h_done")
        sil_ready = sem("sil_ready"); act_ready = sem("act_ready")
        a_hi = sem("a_hi"); a_lo = sem("a_lo")
        arg_ready = sem("arg_ready"); th_ready = sem("th_ready"); wt_ready = sem("wt_ready")
        y_done = sem("y_done"); y_ready = sem("y_ready"); added = sem("added")

        block = ctx.enter_context(nc.Block())

        SCATTERS = 16 * TILES * TOPK
        W_LOADS = 16 * 4
        HT = NH * 2
        LAYERS = [(raw_b, hi_b, lo_b), (raw_a, hi_a, lo_a), (raw_2, hi_2, lo_2)]
        BLOCKS = [(c, j) for c in range(2) for j in range(NH)]
        FULL = (SLOT_TILES - 1) * P

        def alone(eng):
            eng.sem_inc(passed, 1)

        def experts(eng, run):
            run(0, 0, 0, True, False)
            with eng.Fori(0, (E - 2) // 2) as j:
                run(j * 2 + 1, j, 1, False, False)
                run(j * 2 + 2, j + 1, 0, False, False)
            run(E - 1, (E - 1) // 2, (E - 1) % 2, False, True)

        @block.sync
        def _(sp):
            xv = x.rearrange("(t p) c -> p t c", p=P)
            ov = out[0:TOKENS, :].rearrange("(t p) c -> p t c", p=P)
            sp.dma_start(xt[:, 0:TILES, :], xv[:, 0:TILES, :]).then_inc(x_first, 16)
            sp.dma_start(cst[:, :], consts).then_inc(cst_in, 16)
            sp.dma_start(xt[:, TILES:, :], xv[:, TILES:, :]).then_inc(x_rest, 16)
            sp.dma_start(conv_a[:, :], conv_wt[0:P, :]).then_inc(cst_in, 16)
            sp.dma_start(conv_b[:, :], conv_wt[P:, :]).then_inc(cst_in, 16)
            sp.dma_start(wg_a[:, :], wg[0:P, :]).then_inc(cst_in, 16)
            sp.dma_start(wg_b[:, :], wg[P:, :]).then_inc(cst_in, 16)

            def load_weights(e, b):
                w1e = w1[bass.ds(e, 1), :, :].rearrange("e k n -> (e k) n")
                w2e = w2[bass.ds(e, 1), :, :].rearrange("e (k p) n -> (e p) k n", p=P)
                sp.dma_start(raw_b[b][0:CB, :], w1e[P:C, :]).then_inc(w_in[b], 16)
                sp.dma_start(raw_b[b][CB:P, :], w1e[P:C, :]).then_inc(w_in[b], 16)
                sp.dma_start(raw_a[b][:, :], w1e[0:P, :]).then_inc(w_in[b], 16)
                sp.dma_start(raw_2[b][:, :].rearrange("p (k n) -> p k n", k=NH), w2e).then_inc(w_in[b], 16)

            def load_rows(e, b):
                te = table[bass.ds(e * SLOTS, SLOTS), :].rearrange("(t p) r -> p t r", p=P)
                sp.dma_start(rows[b][:, :, 0:C], te[:, :, 0:C]).then_inc(rows_in[b], 16)
                sp.dma_start(rows[b][:, :, C:], te[:, :, P:]).then_inc(rows_in[b], 16)

            def gram_round(g, first):
                sp.wait_ge(gram_sb, g + 1)
                flat = gram_dram[bass.ds(g, 1), :, :].rearrange("g t n -> (g t) n")
                sp.dma_start(flat[:, 0:P * WIN].rearrange("t (p w) -> p t w", w=WIN),
                             gram[:, :, :]).then_inc(gram_out, 16)
                sp.wait_ge(gram_out, 16 * (g + 1))
                if not first:
                    sp.wait_ge(corr_ready, g)
                sp.dma_start(near[:, :, :],
                             flat.rearrange("t (p s) -> p t s", s=SKEW)[:, :, 0:SPAN]).then_inc(near_in, 16)

            def store_x1(g):
                sp.wait_ge(x1_ready, g + 1)
                sp.dma_start(ov[:, bass.ds(g * TILES, TILES), :],
                             xt[:, bass.ds(g * TILES, TILES), :]).then_inc(x1_out, 16)

            gram_round(0, True)
            load_weights(0, 0)
            load_weights(1, 1)
            with sp.Fori(0, GROUPS - 1) as i:
                store_x1(i)
                gram_round(i + 1, False)
            store_x1(GROUPS - 1)

            sp.wait_ge(table_out, 16 * E + SCATTERS * GROUPS)
            load_rows(0, 0)

            def expert(e, half, b, first, last):
                if last:
                    return
                if not first:
                    sp.wait_ge(w_hi, 3 * e)
                    sp.wait_ge(w_lo, 3 * e)
                    load_weights(e + 1, 1 - b)
                    sp.wait_ge(added, 16 * SLOT_TILES * e)
                load_rows(e + 1, 1 - b)

            experts(sp, expert)
            sp.wait_ge(x1_out, 16 * GROUPS)
            sp.wait_ge(added, 16 * SLOT_TILES * E)

        @block.gpsimd
        def _(pool):
            pool.wait_ge(cst_ready, 5)
            for e in range(E):
                pool.dma_start(table[e * SLOTS:(e + 1) * SLOTS, :].rearrange("(t p) r -> p t r", p=P),
                               empty[:, :, :]).then_inc(table_out, 16)

            def copy_f(g, first):
                pool.wait_ge(f_ready, g + 1)
                if not first:
                    pool.wait_ge(c_turned, g)
                    alone(pool)
                nc.gpsimd.tensor_copy(fc[:, :, 0:CB], f[:, :, P:C]).then_inc(fc_copied, 1)

            def scatter(g):
                pool.wait_ge(slot_ready, g + 1)
                pool.wait_ge(table_out, 16 * E + SCATTERS * g)
                alone(pool)
                for t in range(TILES):
                    for k in range(TOPK):
                        n = t * TOPK + k
                        nc.gpsimd.indirect_dma_start(
                            out=table, out_offset=bass.IndirectOffsetOnAxis(ap=slot[:, n:n + 1], axis=0),
                            in_=row[:, t, :], in_offset=None,
                            bounds_check=E * SLOTS - 1, oob_is_err=False).then_inc(table_out, 16)

            def split_lo(e, half, b, first):
                for n, (raw, hi, lo) in enumerate(LAYERS):
                    pool.wait_ge(w_hi, 3 * e + n + 1)
                    nc.gpsimd.tensor_tensor(lo[b][:, :], raw[b][:, :], hi[b][:, :].bitcast(F32),
                                            ALU.subtract).then_inc(w_lo, 1)

            copy_f(0, True)
            split_lo(0, 0, 0, True)
            with pool.Fori(0, GROUPS - 1) as i:
                copy_f(i + 1, False)
                scatter(i)
            scatter(GROUPS - 1)

            def expert(e, half, b, first, last):
                if not last:
                    split_lo(e + 1, half, 1 - b, False)
                for t in range(SLOT_TILES):
                    m = min(P, USED - t * P)
                    pool.wait_ge(y_ready, SLOT_TILES * e + t + 1)
                    if t == 0 and first:
                        pool.wait_ge(x1_out, 16 * GROUPS)
                    if t == 0 and not first:
                        pool.wait_ge(added, 16 * SLOT_TILES * e)
                    alone(pool)
                    nc.gpsimd.indirect_dma_start(
                        out=out, out_offset=bass.IndirectOffsetOnAxis(
                            ap=rows[b][0:m, t, C + CB:C + CB + 1].bitcast(U32), axis=0),
                        in_=y[0:m, t, :], in_offset=None, compute_op=ALU.add).then_inc(added, 16)

            experts(pool, expert)

        @block.scalar
        def _(s):
            def turn_out_a(g, first):
                s.wait_ge(var_a, g + 1)
                nc.scalar.activation(sd_a[:, :], mv_a[:, :, 1], ACT.Sqrt, bias=eps_c[:, :]).then_inc(sqrt_a, 1)
                nc.scalar.activation(len_a[:, :], mv_a[:, :, 1], ACT.Sqrt, scale=float(C)).then_inc(sqrt_a, 1)

            def features_a(g, first):
                s.wait_ge(f_turned, g + 1)
                if not first:
                    s.wait_ge(conv_done, g)
                nc.scalar.copy(ft_a[:, REACH:REACH + GROUP], bank[0][:, :]).then_inc(ft_ready, 1)
                nc.scalar.copy(ft_b[:, REACH:REACH + GROUP], bank[1][0:CB, :]).then_inc(ft_ready, 1)

            def gram_a(g, first):
                if not first:
                    s.wait_ge(gram_out, 16 * g)
                s.wait_ge(gram_done, g + 1)
                for h in range(2):
                    last = nc.scalar.copy(gram[:, 2 * h:2 * h + 2, :],
                                          bank[2 + h][:, :].rearrange("p (t w) -> p t w", t=2)[:, :, 0:WIN])
                last.then_inc(gram_sb, 1)

            def corr_b(g):
                s.wait_ge(c_turned, g + 1)
                nc.scalar.copy(ct[:, :], bank[4][0:CB + NCORR + 1, :]).then_inc(ct_ready, 1)

            def sqrt_of_b(g):
                s.wait_ge(var_b, g + 1)
                nc.scalar.activation(sd_b[:, :], mv_b[:, :, 1], ACT.Sqrt, bias=eps_t[:, :]).then_inc(sqrt_b, 1)

            def tokens_b(g):
                s.wait_ge(t_turned, g + 1)
                nc.scalar.copy(tt_a[:, :], bank[7][:, :])
                nc.scalar.copy(tt_b[:, :], bank[4][0:CB, :]).then_inc(tt_ready, 1)

            def split_hi(e, half, b, which):
                raw, hi, _ = LAYERS[which]
                if which == 0:
                    s.wait_ge(w_in[b], W_LOADS * (half + 1))
                nc.scalar.copy(hi[b][:, :], raw[b][:, :]).then_inc(w_hi, 1)

            s.wait_ge(cst_ready, 5)
            turn_out_a(0, True)
            features_a(0, True)
            gram_a(0, True)
            for which in range(3):
                split_hi(0, 0, 0, which)
            with s.Fori(0, GROUPS - 1) as i:
                turn_out_a(i + 1, False)
                corr_b(i)
                features_a(i + 1, False)
                sqrt_of_b(i)
                gram_a(i + 1, False)
                tokens_b(i)
            corr_b(GROUPS - 1)
            sqrt_of_b(GROUPS - 1)
            tokens_b(GROUPS - 1)

            def slots_hi(e, go):
                s.wait_ge(rows_turned, 2 * e + go + 1)
                if go == 0:
                    nc.scalar.copy(xh_a[:, 0:FULL], bank[6][:, :]).then_inc(x_hi, 1)
                    nc.scalar.copy(x_b[:, 0:FULL], bank[7][:, :]).then_inc(x_hi, 1)
                else:
                    nc.scalar.copy(xh_a[:, FULL:USED], bank[6][:, 0:USED - FULL]).then_inc(x_hi, 1)
                    nc.scalar.copy(x_b[:, FULL:USED], bank[6][:, P:P + USED - FULL]).then_inc(x_hi, 1)

            slots_hi(0, 0)
            slots_hi(0, 1)

            def expert(e, half, b, first, last):
                s.wait_ge(arg_ready, e + 1)
                nc.scalar.activation(th[:, :], arg[:, :], ACT.Tanh, scale=0.5).then_inc(th_ready, 1)

                def hidden_hi(n):
                    c, j = BLOCKS[n]
                    lo, hi = CHUNKS[c]
                    s.wait_ge(act_ready, HT * e + n + 1)
                    nc.scalar.copy(ah[:, j, lo:hi], act[n % 3][:, 0:hi - lo]).then_inc(a_hi, 1)

                for n, (c, j) in enumerate(BLOCKS):
                    lo, hi = CHUNKS[c]
                    s.wait_ge(h_done, HT * e + n + 1)
                    if n >= 2 or not first:
                        s.wait_ge(act_ready, HT * e + n - 1)
                    nc.scalar.activation(sil[n % 2][:, 0:hi - lo], bank[2 * (n % 2) + 1][:, 0:hi - lo],
                                         ACT.Silu).then_inc(sil_ready, 1)
                    if n >= 1:
                        hidden_hi(n - 1)
                    if n in (1, 3, 5) and not last:
                        if n == 1 and not first:
                            s.wait_ge(y_done, SLOT_TILES * e)
                        split_hi(e + 1, half if b == 0 else half + 1, 1 - b, (n - 1) // 2)
                hidden_hi(HT - 1)
                if not last:
                    slots_hi(e + 1, 0)
                    slots_hi(e + 1, 1)

            experts(s, expert)

        @block.vector
        def _(v):
            V = nc.vector
            V.memset(eps_c[:, :], 1e-6)
            V.memset(eps_t[:, :], 1e-5)
            V.memset(ft_a[:, :], 0.0).then_inc(cst_ready, 1)
            V.memset(ft_b[:, :], 0.0).then_inc(cst_ready, 1)
            V.memset(ones[:, :], 1.0)
            V.memset(seen[:, :, :], 0.0)
            V.memset(empty[:, :, :], 0.0).then_inc(cst_ready, 1)
            v.wait_ge(cst_ready, 3)
            v.wait_ge(cst_in, 16 * 5)
            V.tensor_copy(before[:, :], cst[:, C_UPPER:C_UPPER + P]).then_inc(cst_ready, 1)
            V.tensor_copy(empty[:, :, C:C + 1].rearrange("p t o -> p (t o)").bitcast(I32), spare).then_inc(cst_ready, 1)

            def stage_a(g, first):
                step = Count(g * A_STEPS)
                if first:
                    v.wait_ge(x_first, 16)
                else:
                    v.wait_ge(x_rest, 16)
                for t in range(TILES):
                    last = V.bn_stats(stat_a[:, t, :], xt[:, bass.ds(g * TILES + t, 1), :].rearrange("p o c -> p (o c)"))
                last.then_inc(a_step, step.up())
                v.wait_ge(a_step, step.now)
                alone(v)
                for t in range(TILES):
                    last = V.bn_aggr(mv_a[:, t, :], stat_a[:, t, :])
                last.then_inc(var_a, 1)
                v.wait_ge(sqrt_a, 2 * g + 2)
                V.reciprocal(rstd_a[:, :], sd_a[:, :]).then_inc(a_step, step.up())
                v.wait_ge(a_step, step.now)
                V.tensor_tensor(nrm_a[:, :], len_a[:, :], rstd_a[:, :], ALU.mult).then_inc(a_step, step.up())
                v.wait_ge(a_step, step.now)
                V.tensor_scalar(norm[:, bass.ds(g * TILES, TILES)], nrm_a[:, :], 1e-12, None,
                                ALU.max).then_inc(a_step, step.up())
                v.wait_ge(a_step, step.now)
                V.reciprocal(inv_norm[:, bass.ds(g * TILES, TILES)],
                             norm[:, bass.ds(g * TILES, TILES)]).then_inc(a_step, step.up())
                v.wait_ge(a_step, step.now)
                V.tensor_tensor(q_a[:, :], rstd_a[:, :], inv_norm[:, bass.ds(g * TILES, TILES)],
                                ALU.mult).then_inc(f_q, 1)
                v.wait_ge(f_q, g + 1)
                if not first:
                    v.wait_ge(f_turned, g)
                    v.wait_ge(fc_copied, g)
                for t in range(TILES):
                    last = V.tensor_scalar(f[:, t, :], xt[:, bass.ds(g * TILES + t, 1), :].rearrange("p o c -> p (o c)"),
                                           mv_a[:, t, 0:1], q_a[:, t:t + 1], ALU.subtract, ALU.mult)
                last.then_inc(f_ready, 1)
                assert step.n == A_STEPS

            def stage_b(g):
                step = Count(g * B_STEPS)
                gt = bass.ds(g * TILES, TILES)
                v.wait_ge(near_in, 16 * (g + 1))
                for n, (start, pitch) in enumerate([(0, SIDE + 1), (PAD, SIDE),
                                                    (2 * PAD, SIDE - 1), (PAD * SIDE, 1)]):
                    last = V.tensor_tensor(fc[:, :, CB + n * K:CB + (n + 1) * K],
                                           near[:, :, start:start + (K - 1) * pitch + 1:pitch],
                                           mask[:, :, n * K:(n + 1) * K], ALU.mult)
                last.then_inc(b_step, step.up())
                v.wait_ge(b_step, step.now)
                V.tensor_tensor(fc[:, :, CB:CB + NCORR], fc[:, :, CB:CB + NCORR],
                                inv_norm[:, gt].unsqueeze(2).broadcast_to([P, TILES, NCORR]), ALU.mult)
                V.tensor_copy(fc[:, :, CB + NCORR:CB + NCORR + 1], inv_norm[:, gt].unsqueeze(2)).then_inc(corr_ready, 1)
                v.wait_ge(conv_done, g + 1)
                for t in range(TILES):
                    xs = xt[:, bass.ds(g * TILES + t, 1), :].rearrange("p o c -> p (o c)")
                    last = V.scalar_tensor_tensor(out=xs, in0=bank[5 + t // 2][:, 256 * (t % 2):256 * (t % 2) + C],
                                                  scalar=norm[:, bass.ds(g * TILES + t, 1)], in1=xs,
                                                  op0=ALU.mult, op1=ALU.add)
                last.then_inc(x1_ready, 1)
                v.wait_ge(x1_ready, g + 1)
                alone(v)
                for t in range(TILES):
                    last = V.bn_stats(stat_b[:, t, :], xt[:, bass.ds(g * TILES + t, 1), :].rearrange("p o c -> p (o c)"))
                last.then_inc(b_step, step.up())
                v.wait_ge(b_step, step.now)
                alone(v)
                for t in range(TILES):
                    last = V.bn_aggr(mv_b[:, t, :], stat_b[:, t, :])
                last.then_inc(var_b, 1)
                v.wait_ge(sqrt_b, g + 1)
                V.reciprocal(rstd_b[:, :], sd_b[:, :]).then_inc(b_step, step.up())
                v.wait_ge(b_step, step.now)
                v.wait_ge(table_out, 16 * E + SCATTERS * g)
                V.tensor_copy(row[:, :, C].bitcast(I32), cst[:, bass.ds(g * TILES + C_TOK, TILES)])
                for t in range(TILES):
                    last = V.tensor_scalar(row[:, t, 0:C], xt[:, bass.ds(g * TILES + t, 1), :].rearrange("p o c -> p (o c)"),
                                           mv_b[:, t, 0:1], rstd_b[:, t:t + 1], ALU.subtract, ALU.mult)
                last.then_inc(tn_ready, 1)
                V.tensor_copy(seen[:, 0, :], seen[:, TILES, :])
                v.wait_ge(logits_done, g + 1)
                V.tensor_copy(lg[:, :, :], bank[5][:, 0:TILES * E].rearrange("p (t e) -> p t e", t=TILES)).then_inc(b_step, step.up())
                v.wait_ge(b_step, step.now)
                src = lg
                for k in range(TOPK):
                    V.tensor_reduce(top[:, :, k:k + 1], src[:, :, :], AX_X, ALU.max).then_inc(b_step, step.up())
                    v.wait_ge(b_step, step.now)
                    V.tensor_tensor(is_top[:, :, :], src[:, :, :], top[:, :, k:k + 1].broadcast_to([P, TILES, E]),
                                    ALU.is_equal).then_inc(b_step, step.up())
                    v.wait_ge(b_step, step.now)
                    V.tensor_tensor(ranked[:, :, :], is_top[:, :, :], rev.unsqueeze(1).broadcast_to([P, TILES, E]),
                                    ALU.mult).then_inc(b_step, step.up())
                    v.wait_ge(b_step, step.now)
                    V.tensor_reduce(pick[:, :, k:k + 1], ranked[:, :, :], AX_X, ALU.max).then_inc(b_step, step.up())
                    v.wait_ge(b_step, step.now)
                    V.tensor_tensor(onehot[:, :, k, :], ranked[:, :, :],
                                    pick[:, :, k:k + 1].broadcast_to([P, TILES, E]), ALU.is_equal).then_inc(b_step, step.up())
                    v.wait_ge(b_step, step.now)
                    if k == 0:
                        V.scalar_tensor_tensor(out=lg2[:, :, :], in0=onehot[:, :, 0, :], scalar=LOWEST, in1=lg[:, :, :],
                                               op0=ALU.mult, op1=ALU.add).then_inc(b_step, step.up())
                        v.wait_ge(b_step, step.now)
                        src = lg2
                V.tensor_tensor(row[:, :, C + 1], top[:, :, 1], top[:, :, 0], ALU.subtract)
                V.scalar_tensor_tensor(out=region[:, :], in0=pick[:, :, :].rearrange("p t k -> p (t k)"),
                                       scalar=-float(SLOTS), in1=koff, op0=ALU.mult, op1=ALU.add)
                for t in range(TILES):
                    V.tensor_tensor(seen[:, t + 1, :], seen[:, t, :],
                                    onehot[:, t, :, :].rearrange("p k e -> p (k e)"), ALU.add).then_inc(choice_ready, 1)
                    v.wait_ge(choice_ready, TILES * g + t + 1)
                v.wait_ge(place_done, g + 1)
                V.tensor_tensor(place_e[:, :, :], bank[6][:, 0:TILES * TOPK * E].rearrange("p (n e) -> p n e", e=E),
                                onehot[:, :, :, :].rearrange("p t k e -> p (t k) e"), ALU.mult).then_inc(b_step, step.up())
                v.wait_ge(b_step, step.now)
                V.tensor_reduce(place[:, :], place_e[:, :, :], AX_X, ALU.add).then_inc(b_step, step.up())
                v.wait_ge(b_step, step.now)
                V.tensor_scalar(miss[:, :], place[:, :], float(CAP), MISS, ALU.is_ge, ALU.mult)
                V.tensor_tensor(slot_f[:, :], place[:, :], region[:, :], ALU.add).then_inc(b_step, step.up())
                v.wait_ge(b_step, step.now)
                V.tensor_tensor(slot[:, :], slot_f[:, :], miss[:, :], ALU.add).then_inc(slot_ready, 1)
                assert step.n == B_STEPS, step.n

            stage_a(0, True)
            with v.Fori(0, GROUPS - 1) as i:
                stage_a(i + 1, False)
                stage_b(i)
            stage_b(GROUPS - 1)

            def slots_lo(e, go):
                a, z = (0, FULL) if go == 0 else (FULL, USED)
                src_b = bank[7] if go == 0 else bank[6]
                off_b = 0 if go == 0 else P
                v.wait_ge(x_hi, 4 * e + 2 * go + 1 + go)
                V.tensor_tensor(xl_a[:, a:z], bank[6][:, 0:z - a], xh_a[:, a:z].bitcast(F32),
                                ALU.subtract).then_inc(x_lo, 1)
                v.wait_ge(x_hi, 4 * e + 2 * go + 2)
                V.tensor_tensor(x_b[CB:P, a:z], src_b[CB:P, off_b:off_b + z - a], x_b[CB:P, a:z].bitcast(F32),
                                ALU.subtract).then_inc(x_lo, 1)

            slots_lo(0, 0)
            slots_lo(0, 1)

            def expert(e, half, b, first, last):
                v.wait_ge(rows_in[b], 32 * (half + 1))
                V.tensor_tensor(arg[:, :], rows[b][:, :, C + CB + 1], sign, ALU.mult).then_inc(arg_ready, 1)
                v.wait_ge(th_ready, e + 1)
                V.tensor_scalar(wt[b][:, :], th[:, :], 0.5, 0.5, ALU.mult, ALU.add).then_inc(wt_ready, 1)

                def hidden_lo(n):
                    c, j = BLOCKS[n]
                    lo, hi = CHUNKS[c]
                    v.wait_ge(a_hi, HT * e + n + 1)
                    V.tensor_tensor(al[:, j, lo:hi], act[n % 3][:, 0:hi - lo], ah[:, j, lo:hi].bitcast(F32),
                                    ALU.subtract).then_inc(a_lo, 1)

                for n, (c, j) in enumerate(BLOCKS):
                    lo, hi = CHUNKS[c]
                    if n >= 3 or not first:
                        v.wait_ge(a_lo, HT * e + n - 2)
                    v.wait_ge(sil_ready, HT * e + n + 1)
                    V.tensor_tensor(act[n % 3][:, 0:hi - lo], bank[2 * (n % 2)][:, 0:hi - lo],
                                    sil[n % 2][:, 0:hi - lo], ALU.mult).then_inc(act_ready, 1)
                    if n >= 1:
                        hidden_lo(n - 1)
                hidden_lo(HT - 1)

                v.wait_ge(wt_ready, e + 1)

                def take_y(t):
                    v.wait_ge(y_done, SLOT_TILES * e + t + 1)
                    m = min(P, USED - t * P)
                    V.tensor_scalar(y[0:m, t, :], bank[4 + t % 2][0:m, 0:C], wt[b][0:m, t:t + 1], None,
                                    ALU.mult).then_inc(y_ready, 1)

                if not first:
                    v.wait_ge(added, 16 * SLOT_TILES * e)
                if last:
                    for t in range(SLOT_TILES):
                        take_y(t)
                    return
                slots_lo(e + 1, 0)
                take_y(0)
                slots_lo(e + 1, 1)
                for t in range(1, SLOT_TILES):
                    take_y(t)

            experts(v, expert)

        @block.tensor
        def _(pe):
            T = nc.tensor

            def turn_f(g):
                pe.wait_ge(f_ready, g + 1)
                for t in range(TILES):
                    T.transpose(bank[0][:, t * P:(t + 1) * P], f[:, t, 0:P], ident)
                    last = T.transpose(bank[1][0:CB, t * P:(t + 1) * P], f[:, t, P:C], ident)
                last.then_inc(f_turned, 1)

            def grams(g):
                pe.wait_ge(ft_ready, 2 * g + 2)
                for t in range(TILES):
                    o = bank[2 + t // 2][:, 256 * (t % 2):256 * (t % 2) + WIN]
                    own = slice(REACH + t * P, REACH + (t + 1) * P)
                    win = slice(t * P, t * P + WIN)
                    T.matmul(o, ft_a[:, own], ft_a[:, win], start=True, stop=False)
                    last = T.matmul(o, ft_b[:, own], ft_b[:, win], start=False, stop=True)
                last.then_inc(gram_done, 1)

            def turn_c(g):
                pe.wait_ge(fc_copied, g + 1)
                pe.wait_ge(corr_ready, g + 1)
                for t in range(TILES):
                    last = T.transpose(bank[4][0:CB + NCORR + 1, t * P:(t + 1) * P], fc[:, t, :], ident)
                last.then_inc(c_turned, 1)

            def conv(g):
                pe.wait_ge(ct_ready, g + 1)
                for t in range(TILES):
                    o = bank[5 + t // 2][:, 256 * (t % 2):256 * (t % 2) + C]
                    T.matmul(o, ft_a[:, REACH + t * P:REACH + (t + 1) * P], conv_a[:, :], start=True, stop=False)
                    last = T.matmul(o, ct[:, t * P:(t + 1) * P], conv_b[:, :], start=False, stop=True)
                last.then_inc(conv_done, 1)

            def gate(g):
                pe.wait_ge(tn_ready, g + 1)
                for t in range(TILES):
                    T.transpose(bank[7][:, t * P:(t + 1) * P], row[:, t, 0:P], ident)
                    last = T.transpose(bank[4][0:CB, t * P:(t + 1) * P], row[:, t, P:C], ident)
                last.then_inc(t_turned, 1)
                pe.wait_ge(tt_ready, g + 1)
                for t in range(TILES):
                    o = bank[5][:, t * E:(t + 1) * E]
                    T.matmul(o, tt_a[:, t * P:(t + 1) * P], wg_a[:, :], start=True, stop=False)
                    last = T.matmul(o, tt_b[:, t * P:(t + 1) * P], wg_b[:, :], start=False, stop=True)
                last.then_inc(logits_done, 1)

            def places(g):
                pe.wait_ge(choice_ready, TILES * (g + 1))
                o = bank[6][:, 0:TILES * TOPK * E]
                T.matmul(o, before[:, :], onehot[:, :, :, :].rearrange("p t k e -> p (t k e)"), start=True, stop=False)
                T.matmul(o, ones[:, :], seen[:, 0:TILES, :].rearrange("p t n -> p (t n)"),
                         start=False, stop=True).then_inc(place_done, 1)

            pe.wait_ge(cst_ready, 5)
            turn_f(0)
            grams(0)
            with pe.Fori(0, GROUPS - 1) as i:
                turn_c(i)
                conv(i)
                turn_f(i + 1)
                grams(i + 1)
                gate(i)
                places(i)
            turn_c(GROUPS - 1)
            conv(GROUPS - 1)
            gate(GROUPS - 1)
            places(GROUPS - 1)

            def turn_rows(e, half, b, go):
                if go == 0:
                    pe.wait_ge(rows_in[b], 32 * (half + 1))
                    for t in range(SLOT_TILES - 1):
                        T.transpose(bank[6][:, t * P:(t + 1) * P], rows[b][:, t, 0:P], ident)
                        last = T.transpose(bank[7][:, t * P:(t + 1) * P], rows[b][:, t, P:P + 2 * CB], ident)
                else:
                    pe.wait_ge(x_lo, 4 * e + 1)
                    T.transpose(bank[6][:, 0:P], rows[b][:, SLOT_TILES - 1, 0:P], ident)
                    last = T.transpose(bank[6][:, P:2 * P], rows[b][:, SLOT_TILES - 1, P:P + 2 * CB], ident)
                last.then_inc(rows_turned, 1)

            turn_rows(0, 0, 0, 0)
            turn_rows(0, 0, 0, 1)

            def expert(e, half, b, first, last):
                pe.wait_ge(w_hi, 3 * e + 3)
                pe.wait_ge(w_lo, 3 * e + 3)
                pe.wait_ge(x_lo, 4 * e + 4)
                for n, (c, j) in enumerate(BLOCKS):
                    lo, hi = CHUNKS[c]
                    if n >= 2 or not first:
                        pe.wait_ge(act_ready, HT * e + n - 1)
                    for half_h in range(2):
                        o = bank[2 * (n % 2) + half_h][:, 0:hi - lo]
                        cols = slice((half_h * NH + j) * P, (half_h * NH + j + 1) * P)
                        T.matmul(o, hi_a[b][:, cols], xh_a[:, lo:hi], start=True, stop=False)
                        T.matmul(o, hi_a[b][:, cols], xl_a[:, lo:hi], start=False, stop=False)
                        T.matmul(o, lo_a[b][:, cols], xh_a[:, lo:hi], start=False, stop=False)
                        T.matmul(o, hi_b[b][:, cols], x_b[:, lo:hi], start=False, stop=False)
                        mm = T.matmul(o, lo_b[b][:, cols], x_b[:, lo:hi], start=False, stop=True)
                    mm.then_inc(h_done, 1)

                def out_tile(t):
                    m = min(P, USED - t * P)
                    pe.wait_ge(a_lo, HT * e + (NH if (t + 1) * P <= CHUNK else HT))
                    if t >= 2 or not first:
                        pe.wait_ge(y_ready, SLOT_TILES * e + t - 1)
                    o = bank[4 + t % 2][0:m, 0:C]
                    cols = slice(t * P, t * P + m)
                    for j in range(NH):
                        w = slice(j * C, (j + 1) * C)
                        T.matmul(o, ah[:, j, cols], hi_2[b][:, w], start=(j == 0), stop=False)
                        T.matmul(o, ah[:, j, cols], lo_2[b][:, w], start=False, stop=False)
                        mm = T.matmul(o, al[:, j, cols], hi_2[b][:, w], start=False, stop=(j == NH - 1))
                    mm.then_inc(y_done, 1)

                if not last:
                    nxt = half if b == 0 else half + 1
                    turn_rows(e + 1, nxt, 1 - b, 0)
                out_tile(0)
                if not last:
                    turn_rows(e + 1, nxt, 1 - b, 1)
                for t in range(1, SLOT_TILES):
                    out_tile(t)

            experts(pe, expert)


def kernel(x, L0_conv_conv_w, L0_conv_conv_b, L0_ffn_Wg, L0_ffn_W1, L0_ffn_W2):
    import concourse.bacc as bacc
    from concourse.bass_utils import run_bass_kernel_spmd

    arrays = {
        "x_tokens": np.ascontiguousarray(np.asarray(x).reshape(IMAGES, C, PIXELS).transpose(0, 2, 1).reshape(TOKENS, C)),
        "conv_wt": np.concatenate([np.asarray(L0_conv_conv_w).T, np.asarray(L0_conv_conv_b)[None, :]]),
        "wg": np.ascontiguousarray(L0_ffn_Wg),
        "w1": np.ascontiguousarray(L0_ffn_W1),
        "w2": np.ascontiguousarray(L0_ffn_W2),
        "consts": constants(),
    }
    nc = bacc.Bacc("TRN2", target_bir_lowering=False, num_devices=1)
    args = [nc.dram_tensor(n, a.shape, mybir.dt.from_np(a.dtype), kind="ExternalInput").ap() for n, a in arrays.items()]
    out = nc.dram_tensor("out", (TOKENS + SLOTS, C), F32, kind="ExternalOutput").ap()
    metaformer_kernel(nc, *args, out)
    r = run_bass_kernel_spmd(nc, [arrays], core_ids=[0])
    got = r.results[0]["out"][0:TOKENS]
    return np.ascontiguousarray(got.reshape(IMAGES, PIXELS, C).transpose(0, 2, 1).reshape(IMAGES, C, SIDE, SIDE))
```

```python
from contextlib import ExitStack

import numpy as np
import concourse.bass as bass
from concourse import mybir

F32 = mybir.dt.float32
F32R = mybir.dt.float32r
BF16 = mybir.dt.bfloat16
I32 = mybir.dt.int32
U32 = mybir.dt.uint32
ALU = mybir.AluOpType
ACT = mybir.ActivationFunctionType
AX_X = mybir.AxisListType.X

P = 128
IMAGES, C, SIDE = 8, 192, 16
PIXELS = SIDE * SIDE
TOKENS = IMAGES * PIXELS
CB = C - P
TILES = 4
GROUP = TILES * P
GROUPS = TOKENS // GROUP
K = 7
PAD = K // 2
NCORR = 4 * K
REACH = PAD * SIDE + PAD
SPAN = 2 * REACH + 1
WIN = P + 2 * REACH
SKEW = WIN + 1
E, TOPK, H = 8, 2, 512
CAP = int(1.2 * TOKENS / E)
SLOT_TILES = -(-TOPK * CAP // P)
SLOTS = SLOT_TILES * P
USED = TOPK * CAP
CHUNKS = [(0, (USED // 2 + 1) // 2 * 2), ((USED // 2 + 1) // 2 * 2, USED)]
CHUNK = CHUNKS[0][1]
ROW = C + 2
NH = H // P
MISS = float(1 << 20)
LOWEST = -3.0e38

C_IDENT = 0
C_UPPER = C_IDENT + P
C_IOTA = C_UPPER + P
C_MASK = C_IOTA + E
C_KOFF = C_MASK + TILES * NCORR
C_TOK = C_KOFF + TILES * TOPK
C_SIGN = C_TOK + GROUPS * TILES
C_SPARE = C_SIGN + SLOT_TILES
C_ALL = C_SPARE + SLOT_TILES


def constants():
    c = np.zeros((P, C_ALL), np.float32)
    p = np.arange(P)
    c[:, C_IDENT:C_IDENT + P] = np.eye(P)
    c[:, C_UPPER:C_UPPER + P] = p[:, None] < p[None, :]
    c[:, C_IOTA:C_IOTA + E] = np.arange(E)
    offsets = [(i, i) for i in range(K)] + [(i, PAD) for i in range(K)]
    offsets += [(i, K - 1 - i) for i in range(K)] + [(PAD, i) for i in range(K)]
    for t in range(TILES):
        pixel = (t * P + p) % PIXELS
        for n, (r, s) in enumerate(offsets):
            y, x = pixel // SIDE + r - PAD, pixel % SIDE + s - PAD
            c[:, C_MASK + t * NCORR + n] = (y >= 0) & (y < SIDE) & (x >= 0) & (x < SIDE)
        for k in range(TOPK):
            c[:, C_KOFF + t * TOPK + k] = k * CAP
    for t in range(GROUPS * TILES):
        c[:, C_TOK + t] = t * P + p
    for t in range(SLOT_TILES):
        c[:, C_SIGN + t] = np.where(t * P + p < CAP, -1.0, 1.0)
        c[:, C_SPARE + t] = TOKENS + t * P + p
    return c


class Count:

    def __init__(self, base):
        self.base, self.n = base, 0

    def up(self):
        self.n += 1
        return 1

    @property
    def now(self):
        return self.base + self.n


def metaformer_kernel(nc, x, conv_wt, wg, w1, w2, consts, out):
    gram_dram = nc.dram_tensor("gram_dram", [GROUPS, TILES, P * SKEW], F32, kind="Internal").ap()
    table = nc.dram_tensor("slot_table", [E * SLOTS, ROW], F32, kind="Internal").ap()

    with ExitStack() as ctx:
        def sb(name, shape, dt=F32):
            return ctx.enter_context(nc.sbuf_tensor(name, shape, dt))

        def sem(name):
            return ctx.enter_context(nc.semaphore(name))

        bank = [ctx.enter_context(nc.psum_tensor(f"bank{i}", [P, 512], F32)) for i in range(8)]

        cst = sb("cst", [P, C_ALL])
        ident = cst[:, C_IDENT:C_IDENT + P]
        iota = cst[:, C_IOTA:C_IOTA + E]
        mask = cst[:, C_MASK:C_KOFF].rearrange("p (t n) -> p t n", t=TILES)
        koff = cst[:, C_KOFF:C_TOK]
        sign = cst[:, C_SIGN:C_SPARE]
        spare = cst[:, C_SPARE:C_ALL]
        before = sb("before", [P, P], BF16)
        ones = sb("ones", [P, P], BF16)
        eps_c = sb("eps_c", [P, 1])
        eps_t = sb("eps_t", [P, 1])
        conv_a = sb("conv_a", [P, C])
        conv_b = sb("conv_b", [CB + NCORR + 1, C])
        wg_a = sb("wg_a", [P, E])
        wg_b = sb("wg_b", [CB, E])
        empty = sb("empty", [P, SLOT_TILES, ROW])

        def pair(name, shape, dt=F32):
            return [sb(f"{name}{b}", shape, dt) for b in range(2)]

        NT = GROUPS * TILES
        xt = sb("xt", [P, NT, C])
        f = pair("f", [P, TILES, C])
        fc = pair("fc", [P, TILES, CB + NCORR + 1])
        ft_a = pair("ft_a", [P, GROUP + 2 * REACH])
        ft_b = pair("ft_b", [CB, GROUP + 2 * REACH])
        ct = sb("ct", [CB + NCORR + 1, GROUP])
        gram = pair("gram", [P, TILES, WIN])
        near = pair("near", [P, TILES, SPAN])
        picked = sb("picked", [P, TILES, NCORR])
        stat_a = sb("stat_a", [P, NT, 6])
        mv_a = sb("mv_a", [P, NT, 2])
        stat_b = sb("stat_b", [P, NT, 6])
        mv_b = sb("mv_b", [P, NT, 2])
        sd_a = sb("sd_a", [P, NT])
        len_a = sb("len_a", [P, NT])
        rstd_a = sb("rstd_a", [P, NT])
        nrm_a = sb("nrm_a", [P, NT])
        q_a = sb("q_a", [P, NT])
        shift_a = sb("shift_a", [P, NT])
        norm = sb("norm", [P, NT])
        inv_norm = sb("inv_norm", [P, NT])
        sd_b = sb("sd_b", [P, NT])
        rstd_b = sb("rstd_b", [P, NT])
        shift_b = sb("shift_b", [P, NT])
        warm = sb("warm", [P, 1])
        row = [sb(f"row{g}", [P, TILES, ROW]) for g in range(GROUPS)]
        tt_a = sb("tt_a", [P, GROUP])
        tt_b = sb("tt_b", [CB, GROUP])
        top = sb("top", [P, TILES, 8])
        top_e = sb("top_e", [P, TILES, 8], U32)
        pick = sb("pick", [P, TILES, TOPK])
        onehot = sb("onehot", [P, TILES, TOPK, E], BF16)
        seen = sb("seen", [P, GROUPS, TOPK * E], BF16)
        chosen = sb("chosen", [P, TOPK * E])
        place_e = sb("place_e", [P, TILES * TOPK, E])
        place = sb("place", [P, TILES * TOPK])
        miss = sb("miss", [P, TILES * TOPK])
        region = sb("region", [P, TILES * TOPK])
        slot_f = sb("slot_f", [P, TILES * TOPK])
        slot = [sb(f"slot{g}", [P, TILES * TOPK], U32) for g in range(GROUPS)]

        raw_a = [sb(f"raw_a{b}", [P, 2 * H]) for b in range(2)]
        raw_b = [sb(f"raw_b{b}", [P, 2 * H]) for b in range(2)]
        raw_2 = [sb(f"raw_2{b}", [P, NH * C]) for b in range(2)]
        hi_a = [sb(f"hi_a{b}", [P, 2 * H], F32R) for b in range(2)]
        hi_b = [sb(f"hi_b{b}", [P, 2 * H], F32R) for b in range(2)]
        w_2 = [sb(f"w_2{b}", [P, NH, 2, C], F32R) for b in range(2)]
        lo_a = [sb(f"lo_a{b}", [P, 2 * H], F32R) for b in range(2)]
        lo_b = [sb(f"lo_b{b}", [P, 2 * H], F32R) for b in range(2)]
        rows = [sb(f"rows{b}", [P, SLOT_TILES, ROW + CB]) for b in range(2)]
        arg = sb("arg", [P, SLOT_TILES])
        th = sb("th", [P, SLOT_TILES])
        wt = [sb(f"wt{b}", [P, SLOT_TILES]) for b in range(2)]
        xh_a = sb("xh_a", [P, USED], F32R)
        xl_a = sb("xl_a", [P, USED], F32R)
        x_b = sb("x_b", [P, USED], F32R)
        sil = [sb(f"sil{b}", [P, CHUNK]) for b in range(2)]
        act = [sb(f"act{b}", [P, CHUNK]) for b in range(3)]
        ah = sb("ah", [P, NH, USED], F32R)
        al = sb("al", [P, NH, USED], F32R)
        y_part = pair("y_part", [P, C])
        y = sb("y", [P, SLOT_TILES, C])

        x_first = sem("x_first"); x_rest = sem("x_rest")
        cst_in = sem("cst_in"); conv_in = sem("conv_in"); gate_in = sem("gate_in")
        w_in = [sem(f"w_in{b}") for b in range(2)]
        rows_in = [[sem(f"rows_in{b}_{go}") for go in range(2)] for b in range(2)]
        fills = sem("fills"); cst_ready = sem("cst_ready"); before_ready = sem("before_ready"); passed = sem("passed"); v_step = sem("v_step")
        var_a = sem("var_a"); sqrt_a = sem("sqrt_a"); q_ready = sem("q_ready"); f_ready = sem("f_ready")
        fc_copied = sem("fc_copied"); f_turned = sem("f_turned"); ft_ready = sem("ft_ready")
        gram_done = sem("gram_done"); gram_sb = sem("gram_sb")
        gram_out = [[sem(f"gram_out{h}_{b}") for b in range(2)] for h in range(2)]
        near_in = [sem(f"near_in{b}") for b in range(2)]
        corr_ready = sem("corr_ready"); c_turned = sem("c_turned"); ct_ready = sem("ct_ready")
        conv_done = sem("conv_done"); x1_ready = sem("x1_ready"); x1_out = sem("x1_out")
        var_b = sem("var_b"); sqrt_b = sem("sqrt_b"); tn_ready = sem("tn_ready")
        t_turned = sem("t_turned"); tt_ready = sem("tt_ready"); logits_done = sem("logits_done")
        choice_ready = sem("choice_ready"); place_done = sem("place_done"); tn_half = sem("tn_half"); seen_ready = sem("seen_ready"); shift_ready = sem("shift_ready")
        slot_ready = sem("slot_ready"); filled = sem("filled"); table_out = sem("table_out")
        w_hi = sem("w_hi"); w_lo = sem("w_lo"); rows_turned = sem("rows_turned")
        x_hi = sem("x_hi"); x_lo = sem("x_lo"); h_done = sem("h_done")
        sil_ready = sem("sil_ready"); act_ready = sem("act_ready")
        a_hi = sem("a_hi"); a_lo = sem("a_lo")
        arg_ready = sem("arg_ready"); th_ready = sem("th_ready"); wt_ready = sem("wt_ready")
        y_done = sem("y_done"); y_half = sem("y_half"); y_ready = sem("y_ready"); added = sem("added")

        block = ctx.enter_context(nc.Block())

        SCATTERS = 16 * TILES * TOPK
        W_LOADS = 16 * 4
        HT = NH * 2

        def pieces(b):
            r2, w2 = raw_2[b][:, :].rearrange("p (k n) -> p k n", k=NH), w_2[b]
            halves = [slice(0, H), slice(H, 2 * H)]
            return ([(raw_b[b][:, h], hi_b[b][:, h], lo_b[b][:, h]) for h in halves]
                    + [(raw_a[b][:, h], hi_a[b][:, h], lo_a[b][:, h]) for h in halves]
                    + [(r2[:, k, :], w2[:, k, 0, :], w2[:, k, 1, :]) for k in (slice(0, NH // 2), slice(NH // 2, NH))])

        PIECES = 6
        BLOCKS = [(c, j) for c in range(2) for j in range(NH)]
        FRONT_TILES = -(-CHUNK // P)
        FRONT = FRONT_TILES * P
        REST_B = 2 * P
        Y_BANK = [4, 5, 2, 3, 4]
        GO_TILES = [(0, FRONT_TILES), (FRONT_TILES, SLOT_TILES)]

        def alone(eng):
            eng.sem_inc(passed, 1)

        def experts(eng, run):
            run(0, 0, 0, True, False)
            with eng.Fori(0, (E - 2) // 2) as j:
                run(j * 2 + 1, j, 1, False, False)
                run(j * 2 + 2, j + 1, 0, False, False)
            run(E - 1, (E - 1) // 2, (E - 1) % 2, False, True)

        @block.sync
        def _(sp):
            xv = x.rearrange("(t p) c -> p t c", p=P)
            ov = out[0:TOKENS, :].rearrange("(t p) c -> p t c", p=P)
            sp.dma_start(xt[:, 0:TILES, :], xv[:, 0:TILES, :]).then_inc(x_first, 16)
            sp.dma_start(cst[:, :], consts).then_inc(cst_in, 16)
            sp.dma_start(xt[:, TILES:, :], xv[:, TILES:, :]).then_inc(x_rest, 16)
            sp.dma_start(conv_a[:, :], conv_wt[0:P, :]).then_inc(conv_in, 16)
            sp.dma_start(conv_b[:, :], conv_wt[P:, :]).then_inc(conv_in, 16)
            sp.dma_start(wg_a[:, :], wg[0:P, :]).then_inc(gate_in, 16)
            sp.dma_start(wg_b[:, :], wg[P:, :]).then_inc(gate_in, 16)

            def load_weights(e, b):
                w1e = w1[bass.ds(e, 1), :, :].rearrange("e k n -> (e k) n")
                w2e = w2[bass.ds(e, 1), :, :].rearrange("e (k p) n -> (e p) k n", p=P)
                sp.dma_start(raw_b[b][0:CB, :], w1e[P:C, :]).then_inc(w_in[b], 16)
                sp.dma_start(raw_b[b][CB:P, :], w1e[P:C, :]).then_inc(w_in[b], 16)
                sp.dma_start(raw_a[b][:, :], w1e[0:P, :]).then_inc(w_in[b], 16)
                sp.dma_start(raw_2[b][:, :].rearrange("p (k n) -> p k n", k=NH), w2e).then_inc(w_in[b], 16)

            def load_rows(e, b):
                te = table[bass.ds(e * SLOTS, SLOTS), :].rearrange("(t p) r -> p t r", p=P)
                for go, (first, last) in enumerate(GO_TILES):
                    sp.dma_start(rows[b][:, first:last, 0:C], te[:, first:last, 0:C]).then_inc(rows_in[b][go], 16)
                    sp.dma_start(rows[b][:, first:last, C:], te[:, first:last, P:]).then_inc(rows_in[b][go], 16)

            def gram_round(g):
                b, turn = g % 2, g // 2
                for h in range(2):
                    sp.wait_ge(gram_sb, 2 * g + h + 1)
                    sp.dma_start(gram_dram[g, 2 * h:2 * h + 2, 0:P * WIN].rearrange("t (p w) -> p t w", w=WIN),
                                 gram[b][:, 2 * h:2 * h + 2, :]).then_inc(gram_out[h][b], 16)
                if g >= 2:
                    sp.wait_ge(corr_ready, g - 1)
                for h in range(2):
                    sp.wait_ge(gram_out[h][b], 16 * (turn + 1))
                    sp.dma_start(near[b][:, 2 * h:2 * h + 2, :],
                                 gram_dram[g, 2 * h:2 * h + 2, :].rearrange("t (p s) -> p t s", s=SKEW)[:, :, 0:SPAN]
                                 ).then_inc(near_in[b], 16)

            def store_x1(g):
                sp.wait_ge(x1_ready, g + 1)
                tiles = slice(g * TILES, (g + 1) * TILES)
                sp.dma_start(ov[:, tiles, :], xt[:, tiles, :]).then_inc(x1_out, 16)

            AHEAD = 3
            for g in range(AHEAD):
                gram_round(g)
            load_weights(0, 0)
            for g in range(GROUPS):
                store_x1(g)
                if g + AHEAD < GROUPS:
                    gram_round(g + AHEAD)
            load_weights(1, 1)

            sp.wait_ge(table_out, SCATTERS * GROUPS)
            load_rows(0, 0)

            def expert(e, half, b, first, last):
                if last:
                    return
                if not first:
                    sp.wait_ge(w_hi, PIECES * e)
                    sp.wait_ge(w_lo, PIECES * e)
                    load_weights(e + 1, 1 - b)
                    sp.wait_ge(added, 16 * SLOT_TILES * e)
                load_rows(e + 1, 1 - b)

            experts(sp, expert)
            sp.wait_ge(x1_out, 16 * GROUPS)
            sp.wait_ge(added, 16 * SLOT_TILES * E)

        @block.gpsimd
        def _(pool):
            G = nc.gpsimd
            G.memset(eps_c[:, :], 1e-6)
            G.memset(eps_t[:, :], 1e-5)
            for b in range(2):
                for ft in (ft_a, ft_b):
                    G.memset(ft[b][:, 0:REACH], 0.0)
                    G.memset(ft[b][:, REACH + GROUP:], 0.0)
            G.memset(ones[:, :], 1.0)
            G.memset(seen[:, 0, :], 0.0)
            G.memset(empty[:, :, :], 0.0).then_inc(fills, 1)

            EARLY = 5

            def fill_table(first, last):
                if first == 0:
                    pool.wait_ge(cst_in, 16)
                    pool.wait_ge(fills, 1)
                    G.tensor_copy(empty[:, :, C].bitcast(I32), spare).then_inc(cst_ready, 1)
                    pool.wait_ge(cst_ready, 1)
                for e in range(first, last):
                    pool.dma_start(table[e * SLOTS:(e + 1) * SLOTS, :].rearrange("(t p) r -> p t r", p=P),
                                   empty[:, :, :]).then_inc(filled, 16)

            def copy_f(g):
                pool.wait_ge(f_ready, g + 1)
                if g >= 2:
                    pool.wait_ge(c_turned, g - 1)
                G.tensor_copy(fc[g % 2][:, :, 0:CB], f[g % 2][:, :, P:C]).then_inc(fc_copied, 1)

            def scatter(g):
                pool.wait_ge(slot_ready, g + 1)
                if g == 0:
                    pool.wait_ge(filled, 16 * E)
                for t in range(TILES):
                    for k in range(TOPK):
                        n = t * TOPK + k
                        G.indirect_dma_start(
                            out=table, out_offset=bass.IndirectOffsetOnAxis(ap=slot[g][:, n:n + 1], axis=0),
                            in_=row[g][:, t, :], in_offset=None,
                            bounds_check=E * SLOTS - 1, oob_is_err=False).then_inc(table_out, 16)

            def split_lo(e, b):
                for n, (raw, hi, lo) in enumerate(pieces(b)):
                    pool.wait_ge(w_hi, PIECES * e + n + 1)
                    G.tensor_tensor(lo, raw, hi.bitcast(F32), ALU.subtract).then_inc(w_lo, 1)

            fill_table(0, EARLY)
            copy_f(0)
            copy_f(1)
            copy_f(2)
            fill_table(EARLY, E)
            copy_f(3)
            for g in range(GROUPS):
                scatter(g)
            split_lo(0, 0)

            def expert(e, half, b, first, last):
                if not last:
                    split_lo(e + 1, 1 - b)
                for t in range(SLOT_TILES):
                    m = min(P, USED - t * P)
                    pool.wait_ge(y_ready, SLOT_TILES * e + t + 1)
                    if t == 0 and first:
                        pool.wait_ge(x1_out, 16 * GROUPS)
                    if t == 0 and not first:
                        pool.wait_ge(added, 16 * SLOT_TILES * e)
                    alone(pool)
                    nc.gpsimd.indirect_dma_start(
                        out=out, out_offset=bass.IndirectOffsetOnAxis(
                            ap=rows[b][0:m, t, C + CB:C + CB + 1].bitcast(U32), axis=0),
                        in_=y[0:m, t, :], in_offset=None, compute_op=ALU.add).then_inc(added, 16)

            experts(pool, expert)

        @block.scalar
        def _(s):
            def tiles(g):
                return slice(g * TILES, (g + 1) * TILES)

            def deviation(g):
                s.wait_ge(var_a, g + 1)
                nc.scalar.activation(sd_a[:, tiles(g)], mv_a[:, tiles(g), 1], ACT.Sqrt, bias=eps_c[:, :])
                nc.scalar.activation(len_a[:, tiles(g)], mv_a[:, tiles(g), 1], ACT.Sqrt,
                                     scale=float(C)).then_inc(sqrt_a, 1)

            def features(g):
                s.wait_ge(q_ready, g + 1)
                if g >= 2:
                    s.wait_ge(f_turned, g - 1)
                    s.wait_ge(fc_copied, g - 1)
                for t in range(TILES):
                    n = g * TILES + t
                    last = nc.scalar.activation(f[g % 2][:, t, :], xt[:, n, :], ACT.Identity,
                                                bias=shift_a[:, n:n + 1], scale=q_a[:, n:n + 1])
                last.then_inc(f_ready, 1)

            def take_features(g):
                s.wait_ge(f_turned, g + 1)
                if g >= 2:
                    s.wait_ge(conv_done, g - 1)
                nc.scalar.copy(ft_a[g % 2][:, REACH:REACH + GROUP], bank[0][:, :])
                nc.scalar.copy(ft_b[g % 2][:, REACH:REACH + GROUP], bank[1][0:CB, :]).then_inc(ft_ready, 1)

            def take_gram(g):
                for h in range(2):
                    if g >= 2:
                        s.wait_ge(gram_out[h][g % 2], 16 * (g // 2))
                    s.wait_ge(gram_done, 2 * g + h + 1)
                    nc.scalar.copy(gram[g % 2][:, 2 * h:2 * h + 2, :],
                                   bank[2 + h][:, :].rearrange("p (t w) -> p t w", t=2)[:, :, 0:WIN]).then_inc(gram_sb, 1)

            def take_corr(g):
                s.wait_ge(c_turned, g + 1)
                nc.scalar.copy(ct[:, :], bank[5][0:CB + NCORR + 1, :]).then_inc(ct_ready, 1)

            def deviation_b(g):
                s.wait_ge(var_b, g + 1)
                nc.scalar.activation(sd_b[:, tiles(g)], mv_b[:, tiles(g), 1], ACT.Sqrt,
                                     bias=eps_t[:, :]).then_inc(sqrt_b, 1)

            def normed(g):
                s.wait_ge(shift_ready, g + 1)
                for t in range(TILES // 2, TILES):
                    n = g * TILES + t
                    last = nc.scalar.activation(row[g][:, t, 0:C], xt[:, n, :], ACT.Identity,
                                                bias=shift_b[:, n:n + 1], scale=rstd_b[:, n:n + 1])
                last.then_inc(tn_half, 1)

            def take_tokens(g):
                s.wait_ge(t_turned, g + 1)
                nc.scalar.copy(tt_a[:, :], bank[7][:, :])
                nc.scalar.copy(tt_b[:, :], bank[4][0:CB, :]).then_inc(tt_ready, 1)

            def split_hi(half, b, which):
                raw, hi, _ = pieces(b)[which]
                if which == 0:
                    s.wait_ge(w_in[b], W_LOADS * (half + 1))
                nc.scalar.copy(hi, raw).then_inc(w_hi, 1)

            s.wait_ge(fills, 1)
            nc.scalar.activation(warm[:, :], eps_t[:, :], ACT.Sqrt)
            deviation(0)
            features(0)
            deviation(1)
            take_features(0)
            features(1)
            take_gram(0)
            deviation(2)
            take_features(1)
            features(2)
            take_gram(1)
            take_corr(0)
            deviation(3)
            take_features(2)
            features(3)
            for g in range(GROUPS):
                if 1 <= g < GROUPS - 1:
                    take_corr(g + 1)
                deviation_b(g)
                normed(g)
                if g == 0:
                    take_gram(2)
                    take_corr(1)
                take_tokens(g)
                if g == 0:
                    take_features(3)
                    take_gram(3)
                else:
                    split_hi(0, 0, 2 * g - 2)
                    split_hi(0, 0, 2 * g - 1)
            nc.scalar.activation(warm[:, :], eps_t[:, :], ACT.Silu)

            def slots_hi(e, go):
                s.wait_ge(rows_turned, 2 * e + go + 1)
                if go == 0:
                    nc.scalar.copy(xh_a[:, 0:FRONT], bank[6][:, 0:FRONT]).then_inc(x_hi, 1)
                    nc.scalar.copy(x_b[:, 0:FRONT], bank[7][:, 0:FRONT]).then_inc(x_hi, 1)
                else:
                    nc.scalar.copy(xh_a[:, FRONT:USED], bank[6][:, 0:USED - FRONT]).then_inc(x_hi, 1)
                    nc.scalar.copy(x_b[:, FRONT:USED], bank[6][:, REST_B:REST_B + USED - FRONT]).then_inc(x_hi, 1)

            slots_hi(0, 0)

            def expert(e, half, b, first, last):
                s.wait_ge(arg_ready, e + 1)
                nc.scalar.activation(th[:, :], arg[:, :], ACT.Tanh, scale=0.5).then_inc(th_ready, 1)

                def hidden_hi(n):
                    c, j = BLOCKS[n]
                    lo, hi = CHUNKS[c]
                    s.wait_ge(act_ready, HT * e + n + 1)
                    nc.scalar.copy(ah[:, j, lo:hi], act[n % 3][:, 0:hi - lo]).then_inc(a_hi, 1)

                for n, (c, j) in enumerate(BLOCKS):
                    lo, hi = CHUNKS[c]
                    s.wait_ge(h_done, HT * e + n + 1)
                    if n >= 2 or not first:
                        s.wait_ge(act_ready, HT * e + n - 1)
                    nc.scalar.activation(sil[n % 2][:, 0:hi - lo], bank[2 * (n % 2) + 1][:, 0:hi - lo],
                                         ACT.Silu).then_inc(sil_ready, 1)
                    if n >= 1:
                        hidden_hi(n - 1)
                    if first and n == 2:
                        slots_hi(0, 1)
                    if n < PIECES and not last:
                        if n == 0 and not first:
                            s.wait_ge(y_done, SLOT_TILES * e)
                        split_hi(half if b == 0 else half + 1, 1 - b, n)
                hidden_hi(HT - 1)

                def half_y(t):
                    s.wait_ge(y_done, SLOT_TILES * e + t + 1)
                    if t >= 2 or not first:
                        s.wait_ge(y_ready, SLOT_TILES * e + t - 1)
                    m = min(P, USED - t * P)
                    nc.scalar.activation(y_part[t % 2][0:m, :], bank[Y_BANK[t]][0:m, C:2 * C], ACT.Copy,
                                         scale=wt[b][0:m, t:t + 1]).then_inc(y_half, 1)

                s.wait_ge(wt_ready, e + 1)
                if not last:
                    slots_hi(e + 1, 0)
                half_y(0)
                half_y(1)
                if not last:
                    slots_hi(e + 1, 1)
                for t in range(2, SLOT_TILES):
                    half_y(t)

            experts(s, expert)

        @block.vector
        def _(v):
            V = nc.vector
            step = Count(0)

            def tiles(g):
                return slice(g * TILES, (g + 1) * TILES)

            def then(ins):
                ins.then_inc(v_step, step.up())
                v.wait_ge(v_step, step.now)

            def stats(g):
                v.wait_ge(x_first if g == 0 else x_rest, 16)
                for t in range(g * TILES, (g + 1) * TILES):
                    last = V.bn_stats(stat_a[:, t, :], xt[:, t, :])
                then(last)
                for t in range(g * TILES, (g + 1) * TILES):
                    last = V.bn_aggr(mv_a[:, t, :], stat_a[:, t, :])
                last.then_inc(var_a, 1)

            def scales(g):
                n = tiles(g)
                v.wait_ge(sqrt_a, g + 1)
                then(V.reciprocal(rstd_a[:, n], sd_a[:, n]))
                then(V.tensor_tensor(nrm_a[:, n], len_a[:, n], rstd_a[:, n], ALU.mult))
                then(V.tensor_scalar(norm[:, n], nrm_a[:, n], 1e-12, None, ALU.max))
                then(V.reciprocal(inv_norm[:, n], norm[:, n]))
                then(V.tensor_tensor(q_a[:, n], rstd_a[:, n], inv_norm[:, n], ALU.mult))
                V.scalar_tensor_tensor(out=shift_a[:, n], in0=mv_a[:, n, 0], scalar=-1.0, in1=q_a[:, n],
                                       op0=ALU.mult, op1=ALU.mult).then_inc(q_ready, 1)

            def correlations(g):
                b = g % 2
                v.wait_ge(near_in[b], 32 * (g // 2 + 1))
                for n, (start, pitch) in enumerate([(0, SIDE + 1), (PAD, SIDE),
                                                    (2 * PAD, SIDE - 1), (PAD * SIDE, 1)]):
                    last = V.tensor_tensor(picked[:, :, n * K:(n + 1) * K],
                                           near[b][:, :, start:start + (K - 1) * pitch + 1:pitch],
                                           mask[:, :, n * K:(n + 1) * K], ALU.mult)
                if g >= 2:
                    v.wait_ge(c_turned, g - 1)
                V.tensor_copy(fc[b][:, :, CB + NCORR:], inv_norm[:, tiles(g)].unsqueeze(2))
                then(last)
                V.tensor_tensor(fc[b][:, :, CB:CB + NCORR], picked[:, :, :],
                                inv_norm[:, tiles(g)].unsqueeze(2).broadcast_to([P, TILES, NCORR]),
                                ALU.mult).then_inc(corr_ready, 1)

            def residual(g):
                b = g % 2
                v.wait_ge(conv_done, g + 1)
                for t in range(TILES):
                    n = g * TILES + t
                    last = V.scalar_tensor_tensor(out=xt[:, n, :], in0=bank[5 + t // 2][:, 256 * (t % 2):256 * (t % 2) + C],
                                                  scalar=norm[:, n:n + 1], in1=xt[:, n, :],
                                                  op0=ALU.mult, op1=ALU.add)
                last.then_inc(x1_ready, 1)
                v.wait_ge(x1_ready, g + 1)
                for n in range(g * TILES, (g + 1) * TILES):
                    last = V.bn_stats(stat_b[:, n, :], xt[:, n, :])
                then(last)
                for n in range(g * TILES, (g + 1) * TILES):
                    last = V.bn_aggr(mv_b[:, n, :], stat_b[:, n, :])
                last.then_inc(var_b, 1)

            def normed(g):
                v.wait_ge(sqrt_b, g + 1)
                then(V.reciprocal(rstd_b[:, tiles(g)], sd_b[:, tiles(g)]))
                V.scalar_tensor_tensor(out=shift_b[:, tiles(g)], in0=mv_b[:, tiles(g), 0], scalar=-1.0,
                                       in1=rstd_b[:, tiles(g)], op0=ALU.mult, op1=ALU.mult).then_inc(shift_ready, 1)
                V.tensor_copy(row[g][:, :, C].bitcast(I32), cst[:, C_TOK + g * TILES:C_TOK + (g + 1) * TILES])
                for t in range(TILES // 2):
                    n = g * TILES + t
                    last = V.tensor_scalar(row[g][:, t, 0:C], xt[:, n, :], mv_b[:, n, 0:1], rstd_b[:, n:n + 1],
                                           ALU.subtract, ALU.mult)
                last.then_inc(tn_ready, 1)

            def choose(g):
                v.wait_ge(logits_done, g + 1)
                for t in range(TILES):
                    last = V.max(top[:, t, :], bank[7][:, t * E:(t + 1) * E])
                then(last)
                for t in range(TILES):
                    last = V.max_index(top_e[:, t, :], top[:, t, :], bank[7][:, t * E:(t + 1) * E])
                then(last)
                then(V.tensor_copy(pick[:, :, :], top_e[:, :, 0:TOPK]))
                V.tensor_tensor(onehot[:, :, :, :].rearrange("p t k e -> p (t k) e"),
                                iota.unsqueeze(1).broadcast_to([P, TILES * TOPK, E]),
                                pick[:, :, :].rearrange("p t k -> p (t k)").unsqueeze(2).broadcast_to([P, TILES * TOPK, E]),
                                ALU.is_equal).then_inc(choice_ready, 1)
                V.tensor_tensor(row[g][:, :, C + 1], top[:, :, 1], top[:, :, 0], ALU.subtract)
                V.scalar_tensor_tensor(out=region[:, :], in0=pick[:, :, :].rearrange("p t k -> p (t k)"),
                                       scalar=float(SLOTS), in1=koff, op0=ALU.mult, op1=ALU.add)
                if g + 1 < GROUPS:
                    v.wait_ge(choice_ready, g + 1)
                    then(V.tensor_reduce(chosen[:, :], onehot[:, :, :, :].rearrange("p t k e -> p (k e) t"),
                                         AX_X, ALU.add))
                    V.tensor_tensor(seen[:, g + 1, :], seen[:, g, :], chosen[:, :], ALU.add).then_inc(seen_ready, 1)

            def find_slots(g):
                v.wait_ge(place_done, g + 1)
                then(V.tensor_tensor(place_e[:, :, :],
                                     bank[7][:, 2 * P:2 * P + TILES * TOPK * E].rearrange("p (n e) -> p n e", e=E),
                                     onehot[:, :, :, :].rearrange("p t k e -> p (t k) e"), ALU.mult))
                then(V.tensor_reduce(place[:, :], place_e[:, :, :], AX_X, ALU.add))
                V.tensor_scalar(miss[:, :], place[:, :], float(CAP), MISS, ALU.is_ge, ALU.mult)
                then(V.tensor_tensor(slot_f[:, :], place[:, :], region[:, :], ALU.add))
                V.tensor_tensor(slot[g][:, :], slot_f[:, :], miss[:, :], ALU.add).then_inc(slot_ready, 1)

            stats(0)
            scales(0)
            v.wait_ge(fills, 1)
            v.wait_ge(cst_in, 16)
            V.tensor_copy(before[:, :], cst[:, C_UPPER:C_UPPER + P]).then_inc(before_ready, 1)
            for g in (1, 2):
                stats(g)
                scales(g)
            correlations(0)
            stats(3)
            scales(3)
            for g in range(GROUPS):
                residual(g)
                if g + 1 < GROUPS:
                    correlations(g + 1)
                if g >= 1:
                    choose(g - 1)
                    find_slots(g - 1)
                normed(g)
            choose(GROUPS - 1)
            find_slots(GROUPS - 1)

            def slots_lo(e, go):
                a, z = (0, FRONT) if go == 0 else (FRONT, USED)
                src_b = bank[7] if go == 0 else bank[6]
                off_b = 0 if go == 0 else REST_B
                v.wait_ge(x_hi, 4 * e + 2 * go + 1 + go)
                V.tensor_tensor(xl_a[:, a:z], bank[6][:, 0:z - a], xh_a[:, a:z].bitcast(F32),
                                ALU.subtract).then_inc(x_lo, 1)
                v.wait_ge(x_hi, 4 * e + 2 * go + 2)
                V.tensor_tensor(x_b[CB:P, a:z], src_b[CB:P, off_b:off_b + z - a], x_b[CB:P, a:z].bitcast(F32),
                                ALU.subtract).then_inc(x_lo, 1)

            slots_lo(0, 0)

            def expert(e, half, b, first, last):
                for go in range(2):
                    v.wait_ge(rows_in[b][go], 32 * (half + 1))
                V.tensor_tensor(arg[:, :], rows[b][:, :, C + CB + 1], sign, ALU.mult).then_inc(arg_ready, 1)
                v.wait_ge(th_ready, e + 1)
                V.tensor_scalar(wt[b][:, :], th[:, :], 0.5, 0.5, ALU.mult, ALU.add).then_inc(wt_ready, 1)

                def hidden_lo(n):
                    c, j = BLOCKS[n]
                    lo, hi = CHUNKS[c]
                    v.wait_ge(a_hi, HT * e + n + 1)
                    V.tensor_tensor(al[:, j, lo:hi], act[n % 3][:, 0:hi - lo], ah[:, j, lo:hi].bitcast(F32),
                                    ALU.subtract).then_inc(a_lo, 1)

                for n, (c, j) in enumerate(BLOCKS):
                    lo, hi = CHUNKS[c]
                    if n >= 3 or not first:
                        v.wait_ge(a_lo, HT * e + n - 2)
                    v.wait_ge(sil_ready, HT * e + n + 1)
                    V.tensor_tensor(act[n % 3][:, 0:hi - lo], bank[2 * (n % 2)][:, 0:hi - lo],
                                    sil[n % 2][:, 0:hi - lo], ALU.mult).then_inc(act_ready, 1)
                    if n >= 1:
                        hidden_lo(n - 1)
                    if first and n == 2:
                        slots_lo(0, 1)
                hidden_lo(HT - 1)

                v.wait_ge(wt_ready, e + 1)

                def take_y(t):
                    v.wait_ge(y_done, SLOT_TILES * e + t + 1)
                    m = min(P, USED - t * P)
                    v.wait_ge(y_half, SLOT_TILES * e + t + 1)
                    V.scalar_tensor_tensor(out=y[0:m, t, :], in0=bank[Y_BANK[t]][0:m, 0:C],
                                           scalar=wt[b][0:m, t:t + 1], in1=y_part[t % 2][0:m, :],
                                           op0=ALU.mult, op1=ALU.add).then_inc(y_ready, 1)

                if not first:
                    v.wait_ge(added, 16 * SLOT_TILES * e)
                if last:
                    for t in range(SLOT_TILES):
                        take_y(t)
                    return
                slots_lo(e + 1, 0)
                take_y(0)
                take_y(1)
                slots_lo(e + 1, 1)
                for t in range(2, SLOT_TILES):
                    take_y(t)

            experts(v, expert)

        @block.tensor
        def _(pe):
            T = nc.tensor

            BUSY_START, BUSY_FIRST, BUSY, BUSY_BEFORE, BUSY_END = 14, 4, 6, 8, 64

            def keep_busy(n, idle):
                for _ in range(n):
                    T.matmul(idle[:, :], ones[:, :], ones[:, :].unsqueeze(1).broadcast_to([P, 4, P]),
                             start=True, stop=True)

            def turn_f(g):
                if g >= 1:
                    pe.wait_ge(ft_ready, g)
                pe.wait_ge(f_ready, g + 1)
                for t in range(TILES):
                    T.transpose(bank[0][:, t * P:(t + 1) * P], f[g % 2][:, t, 0:P], ident)
                    last = T.transpose(bank[1][0:CB, t * P:(t + 1) * P], f[g % 2][:, t, P:C], ident)
                last.then_inc(f_turned, 1)

            def grams(g):
                pe.wait_ge(ft_ready, g + 1)
                if g >= 1:
                    pe.wait_ge(gram_sb, 2 * g)
                fa, fb = ft_a[g % 2], ft_b[g % 2]
                for t in range(TILES):
                    o = bank[2 + t // 2][:, 256 * (t % 2):256 * (t % 2) + WIN]
                    own = slice(REACH + t * P, REACH + (t + 1) * P)
                    win = slice(t * P, t * P + WIN)
                    T.matmul(o, fa[:, own], fa[:, win], start=True, stop=False)
                    last = T.matmul(o, fb[:, own], fb[:, win], start=False, stop=True)
                    if t % 2:
                        last.then_inc(gram_done, 1)

            def turn_corr(g):
                if g >= 1:
                    pe.wait_ge(x1_ready, g)
                pe.wait_ge(fc_copied, g + 1)
                pe.wait_ge(corr_ready, g + 1)
                for t in range(TILES):
                    last = T.transpose(bank[5][0:CB + NCORR + 1, t * P:(t + 1) * P], fc[g % 2][:, t, :], ident)
                last.then_inc(c_turned, 1)

            def conv(g):
                if g == 0:
                    pe.wait_ge(conv_in, 32)
                pe.wait_ge(ct_ready, g + 1)
                for t in range(TILES):
                    o = bank[5 + t // 2][:, 256 * (t % 2):256 * (t % 2) + C]
                    T.matmul(o, ft_a[g % 2][:, REACH + t * P:REACH + (t + 1) * P], conv_a[:, :], start=True, stop=False)
                    last = T.matmul(o, ct[:, t * P:(t + 1) * P], conv_b[:, :], start=False, stop=True)
                last.then_inc(conv_done, 1)

            def turn_tokens(g):
                pe.wait_ge(tn_ready, g + 1)
                pe.wait_ge(tn_half, g + 1)
                if g >= 1:
                    pe.wait_ge(slot_ready, g)
                for t in range(TILES):
                    T.transpose(bank[7][:, t * P:(t + 1) * P], row[g][:, t, 0:P], ident)
                    last = T.transpose(bank[4][0:CB, t * P:(t + 1) * P], row[g][:, t, P:C], ident)
                last.then_inc(t_turned, 1)

            def logits(g):
                if g == 0:
                    pe.wait_ge(gate_in, 32)
                pe.wait_ge(tt_ready, g + 1)
                for t in range(TILES):
                    o = bank[7][:, t * E:(t + 1) * E]
                    T.matmul(o, tt_a[:, t * P:(t + 1) * P], wg_a[:, :], start=True, stop=False)
                    last = T.matmul(o, tt_b[:, t * P:(t + 1) * P], wg_b[:, :], start=False, stop=True)
                last.then_inc(logits_done, 1)

            def places(g):
                if g == 0:
                    pe.wait_ge(before_ready, 1)
                pe.wait_ge(choice_ready, g + 1)
                o = bank[7][:, 2 * P:2 * P + TILES * TOPK * E]
                picks = onehot[:, :, :, :].rearrange("p t k e -> p (t k e)")
                T.matmul(o, before[:, :], picks, start=True, stop=False)
                for d in range(1, TILES):
                    n = d * TOPK * E
                    T.matmul(o[:, n:], ones[:, :], picks[:, 0:TILES * TOPK * E - n], start=False, stop=False,
                             skip_group_check=True)
                if g >= 1:
                    pe.wait_ge(seen_ready, g)
                T.matmul(o, ones[:, :], seen[:, g, :].unsqueeze(1).broadcast_to([P, TILES, TOPK * E]),
                         start=False, stop=True).then_inc(place_done, 1)

            pe.wait_ge(fills, 1)
            keep_busy(BUSY_START, bank[0])
            pe.wait_ge(cst_in, 16)
            for g in (0, 1):
                turn_f(g)
                grams(g)
            turn_f(2)
            keep_busy(BUSY_FIRST, bank[7])
            turn_corr(0)
            conv(0)
            grams(2)
            for g in range(GROUPS):
                if g + 1 < GROUPS:
                    turn_corr(g + 1)
                if g == 0:
                    turn_tokens(0)
                if g >= 1:
                    places(g - 1)
                if g + 1 < GROUPS:
                    conv(g + 1)
                if g == GROUPS - 1:
                    keep_busy(BUSY_BEFORE, bank[0])
                if g >= 1:
                    turn_tokens(g)
                    keep_busy(BUSY, bank[0])
                else:
                    turn_f(3)
                logits(g)
                if g == 0:
                    grams(3)
            keep_busy(BUSY, bank[0])
            places(GROUPS - 1)
            keep_busy(BUSY_END, bank[0])

            def turn_rows(e, half, b, go):
                pe.wait_ge(rows_in[b][go], 32 * (half + 1))
                if go == 1:
                    pe.wait_ge(x_lo, 4 * e + 1)
                bank_b, off_b = (bank[7], 0) if go == 0 else (bank[6], REST_B)
                first, end = GO_TILES[go]
                for t in range(first, end):
                    at = (t - first) * P
                    T.transpose(bank[6][:, at:at + P], rows[b][:, t, 0:P], ident)
                    last = T.transpose(bank_b[:, off_b + at:off_b + at + P], rows[b][:, t, P:P + 2 * CB], ident)
                last.then_inc(rows_turned, 1)

            turn_rows(0, 0, 0, 0)

            def expert(e, half, b, first, last):
                pe.wait_ge(w_hi, PIECES * (e + 1))
                pe.wait_ge(w_lo, PIECES * (e + 1))
                for n, (c, j) in enumerate(BLOCKS):
                    lo, hi = CHUNKS[c]
                    if first and n == 2:
                        turn_rows(0, 0, 0, 1)
                    if n >= 2 or not first:
                        pe.wait_ge(act_ready, HT * e + n - 1)
                    if n == 1 and not first:
                        pe.wait_ge(y_ready, SLOT_TILES * e - 1)
                    for half_h in range(2):
                        o = bank[2 * (n % 2) + half_h][:, 0:hi - lo]
                        cols = slice((half_h * NH + j) * P, (half_h * NH + j + 1) * P)
                        if j == 0 and half_h == 0:
                            pe.wait_ge(x_hi, 4 * e + 2 * c + 1)
                        T.matmul(o, hi_a[b][:, cols], xh_a[:, lo:hi], start=True, stop=False)
                        T.matmul(o, lo_a[b][:, cols], xh_a[:, lo:hi], start=False, stop=False)
                        if j == 0 and half_h == 0:
                            pe.wait_ge(x_lo, 4 * e + 2 * c + 1)
                        T.matmul(o, hi_a[b][:, cols], xl_a[:, lo:hi], start=False, stop=False)
                        if j == 0 and half_h == 0:
                            pe.wait_ge(x_lo, 4 * e + 2 * c + 2)
                        T.matmul(o, hi_b[b][:, cols], x_b[:, lo:hi], start=False, stop=False)
                        mm = T.matmul(o, lo_b[b][:, cols], x_b[:, lo:hi], start=False, stop=True)
                    mm.then_inc(h_done, 1)

                def out_tile(t):
                    m = min(P, USED - t * P)
                    pe.wait_ge(a_lo, HT * e + (NH if (t + 1) * P <= CHUNK else HT))
                    if t == 0 and not first:
                        pe.wait_ge(y_ready, SLOT_TILES * e)
                    if t == 4:
                        pe.wait_ge(y_ready, SLOT_TILES * e + 1)
                    acc = bank[Y_BANK[t]][0:m, 0:2 * C]
                    cols = slice(t * P, t * P + m)
                    for j in range(NH):
                        T.matmul(acc, ah[:, j, cols], w_2[b][:, j, :, :].rearrange("p h n -> p (h n)"),
                                 start=(j == 0), stop=(j == NH - 1))
                        mm = T.matmul(acc[:, 0:C], al[:, j, cols], w_2[b][:, j, 0, :],
                                      start=False, stop=(j == NH - 1), skip_group_check=True)
                    mm.then_inc(y_done, 1)

                if not last:
                    nxt = half if b == 0 else half + 1
                    turn_rows(e + 1, nxt, 1 - b, 0)
                out_tile(0)
                out_tile(1)
                if not last:
                    turn_rows(e + 1, nxt, 1 - b, 1)
                for t in range(2, SLOT_TILES):
                    out_tile(t)

            experts(pe, expert)


def kernel(x, L0_conv_conv_w, L0_conv_conv_b, L0_ffn_Wg, L0_ffn_W1, L0_ffn_W2):
    import concourse.bacc as bacc
    from concourse.bass_utils import run_bass_kernel_spmd

    arrays = {
        "x_tokens": np.ascontiguousarray(np.asarray(x).reshape(IMAGES, C, PIXELS).transpose(0, 2, 1).reshape(TOKENS, C)),
        "conv_wt": np.concatenate([np.asarray(L0_conv_conv_w).T, np.asarray(L0_conv_conv_b)[None, :]]),
        "wg": np.ascontiguousarray(L0_ffn_Wg),
        "w1": np.ascontiguousarray(L0_ffn_W1),
        "w2": np.ascontiguousarray(L0_ffn_W2),
        "consts": constants(),
    }
    nc = bacc.Bacc("TRN2", target_bir_lowering=False, num_devices=1)
    args = [nc.dram_tensor(n, a.shape, mybir.dt.from_np(a.dtype), kind="ExternalInput").ap() for n, a in arrays.items()]
    out = nc.dram_tensor("out", (TOKENS + SLOTS, C), F32, kind="ExternalOutput").ap()
    metaformer_kernel(nc, *args, out)
    r = run_bass_kernel_spmd(nc, [arrays], core_ids=[0])
    got = r.results[0]["out"][0:TOKENS]
    return np.ascontiguousarray(got.reshape(IMAGES, PIXELS, C).transpose(0, 2, 1).reshape(IMAGES, C, SIDE, SIDE))
```

```python
from contextlib import ExitStack

import numpy as np
import concourse.bass as bass
from concourse import mybir

F32 = mybir.dt.float32
F32R = mybir.dt.float32r
BF16 = mybir.dt.bfloat16
I32 = mybir.dt.int32
U32 = mybir.dt.uint32
ALU = mybir.AluOpType
ACT = mybir.ActivationFunctionType
AX_X = mybir.AxisListType.X

P = 128
IMAGES, C, SIDE = 8, 192, 16
PIXELS = SIDE * SIDE
TOKENS = IMAGES * PIXELS
CB = C - P
TILES = 4
GROUP = TILES * P
GROUPS = TOKENS // GROUP
K = 7
PAD = K // 2
NCORR = 4 * K
REACH = PAD * SIDE + PAD
SPAN = 2 * REACH + 1
WIN = P + 2 * REACH
SKEW = WIN + 1
E, TOPK, H = 8, 2, 512
CAP = int(1.2 * TOKENS / E)
CHUNK = CAP + CAP % 2
CHUNKS = [(0, CHUNK), (CHUNK, 2 * CHUNK)]
USED = TOPK * CHUNK
SLOT_TILES = -(-USED // P)
SLOTS = SLOT_TILES * P
FRONT_TILES = -(-CHUNK // P)
EDGE = CHUNK % P
LIST = -(-(SLOTS - CHUNK) // 16) * 16
ROW = C + 2
NH = H // P
MISS = float(1 << 20)
NO_TOKEN = float(1 << 20)
LOWEST = -3.0e38

C_IDENT = 0
C_UPPER = C_IDENT + P
C_IOTA = C_UPPER + P
C_MASK = C_IOTA + E
C_TOK = C_MASK + TILES * NCORR
C_SIGN = C_TOK + GROUPS * TILES
C_SPARE = C_SIGN + SLOT_TILES
C_ALL = C_SPARE + SLOT_TILES


def constants():
    c = np.zeros((P, C_ALL), np.float32)
    p = np.arange(P)
    c[:, C_IDENT:C_IDENT + P] = np.eye(P)
    c[:, C_UPPER:C_UPPER + P] = p[:, None] < p[None, :]
    c[:, C_IOTA:C_IOTA + E] = np.arange(E)
    offsets = [(i, i) for i in range(K)] + [(i, PAD) for i in range(K)]
    offsets += [(i, K - 1 - i) for i in range(K)] + [(PAD, i) for i in range(K)]
    for t in range(TILES):
        pixel = (t * P + p) % PIXELS
        for n, (r, s) in enumerate(offsets):
            y, x = pixel // SIDE + r - PAD, pixel % SIDE + s - PAD
            c[:, C_MASK + t * NCORR + n] = (y >= 0) & (y < SIDE) & (x >= 0) & (x < SIDE)
    for t in range(GROUPS * TILES):
        c[:, C_TOK + t] = t * P + p
    for t in range(SLOT_TILES):
        c[:, C_SIGN + t] = np.where(t * P + p < CHUNK, -1.0, 1.0)
        c[:, C_SPARE + t] = TOKENS + t * P + p
    return c


class Count:

    def __init__(self, base):
        self.base, self.n = base, 0

    def up(self):
        self.n += 1
        return 1

    @property
    def now(self):
        return self.base + self.n


def metaformer_kernel(nc, x, conv_wt, wg, w1, w2, consts, out):
    gram_dram = nc.dram_tensor("gram_dram", [GROUPS, TILES, P * SKEW], F32, kind="Internal").ap()
    table = [nc.dram_tensor(f"slot_table{k}", [E * LIST, ROW], F32, kind="Internal").ap() for k in range(TOPK)]

    with ExitStack() as ctx:
        def sb(name, shape, dt=F32):
            return ctx.enter_context(nc.sbuf_tensor(name, shape, dt))

        def sem(name):
            return ctx.enter_context(nc.semaphore(name))

        bank = [ctx.enter_context(nc.psum_tensor(f"bank{i}", [P, 512], F32)) for i in range(8)]

        cst = sb("cst", [P, C_ALL])
        ident = cst[:, C_IDENT:C_IDENT + P]
        iota = cst[:, C_IOTA:C_IOTA + E]
        mask = cst[:, C_MASK:C_TOK].rearrange("p (t n) -> p t n", t=TILES)
        sign = cst[:, C_SIGN:C_SPARE]
        spare = cst[:, C_SPARE:C_ALL]
        before = sb("before", [P, P], BF16)
        ones = sb("ones", [P, P], BF16)
        eps_c = sb("eps_c", [P, 1])
        eps_t = sb("eps_t", [P, 1])
        conv_a = sb("conv_a", [P, C])
        conv_b = sb("conv_b", [CB + NCORR + 1, C])
        wg_a = sb("wg_a", [P, E])
        wg_b = sb("wg_b", [CB, E])
        FILLS = 3
        empty = sb("empty", [P, E * LIST // P // FILLS, ROW])

        def pair(name, shape, dt=F32):
            return [sb(f"{name}{b}", shape, dt) for b in range(2)]

        NT = GROUPS * TILES
        xt = sb("xt", [P, NT, C])
        f = pair("f", [P, TILES, C])
        fc = pair("fc", [P, TILES, CB + NCORR + 1])
        ft_a = pair("ft_a", [P, GROUP + 2 * REACH])
        ft_b = pair("ft_b", [CB, GROUP + 2 * REACH])
        ct = sb("ct", [CB + NCORR + 1, GROUP])
        gram = pair("gram", [P, TILES, WIN])
        near = pair("near", [P, TILES, SPAN])
        picked = sb("picked", [P, TILES, NCORR])
        stat_a = sb("stat_a", [P, NT, 6])
        mv_a = sb("mv_a", [P, NT, 2])
        stat_b = sb("stat_b", [P, NT, 6])
        mv_b = sb("mv_b", [P, NT, 2])
        sd_a = sb("sd_a", [P, NT])
        len_a = sb("len_a", [P, NT])
        rstd_a = sb("rstd_a", [P, NT])
        nrm_a = sb("nrm_a", [P, NT])
        q_a = sb("q_a", [P, NT])
        shift_a = sb("shift_a", [P, NT])
        norm = sb("norm", [P, NT])
        inv_norm = sb("inv_norm", [P, NT])
        sd_b = sb("sd_b", [P, NT])
        rstd_b = sb("rstd_b", [P, NT])
        shift_b = sb("shift_b", [P, NT])
        warm = sb("warm", [P, 1])
        row = [sb(f"row{g}", [P, TILES, ROW]) for g in range(GROUPS)]
        tt_a = sb("tt_a", [P, GROUP])
        tt_b = sb("tt_b", [CB, GROUP])
        top = sb("top", [P, TILES, 8])
        top_e = sb("top_e", [P, TILES, 8], U32)
        pick = sb("pick", [P, TILES, TOPK])
        onehot = sb("onehot", [P, TILES, TOPK, E], BF16)
        seen = sb("seen", [P, GROUPS, TOPK * E], BF16)
        chosen = sb("chosen", [P, TOPK * E])
        place_e = sb("place_e", [P, TILES * TOPK, E])
        place = sb("place", [P, TILES * TOPK])
        miss = sb("miss", [P, TILES * TOPK])
        slot_f = sb("slot_f", [P, TILES * TOPK])
        slot = [sb(f"slot{g}", [P, TILES * TOPK], U32) for g in range(GROUPS)]

        raw_a = [sb(f"raw_a{b}", [P, 2 * H]) for b in range(2)]
        raw_b = [sb(f"raw_b{b}", [P, 2 * H]) for b in range(2)]
        raw_2 = [sb(f"raw_2{b}", [P, NH * C]) for b in range(2)]
        hi_a = [sb(f"hi_a{b}", [P, 2 * H], F32R) for b in range(2)]
        hi_b = [sb(f"hi_b{b}", [P, 2 * H], F32R) for b in range(2)]
        w_2 = [sb(f"w_2{b}", [P, NH, 2, C], F32R) for b in range(2)]
        lo_a = [sb(f"lo_a{b}", [P, 2 * H], F32R) for b in range(2)]
        lo_b = [sb(f"lo_b{b}", [P, 2 * H], F32R) for b in range(2)]
        rows = [sb(f"rows{b}", [P, SLOT_TILES, ROW + CB]) for b in range(2)]
        arg = sb("arg", [P, SLOT_TILES])
        th = sb("th", [P, SLOT_TILES])
        wt = [sb(f"wt{b}", [P, SLOT_TILES]) for b in range(2)]
        xh_a = sb("xh_a", [P, USED], F32R)
        xl_a = sb("xl_a", [P, USED], F32R)
        x_b = sb("x_b", [P, USED], F32R)
        sil = [sb(f"sil{b}", [P, CHUNK]) for b in range(2)]
        act = [sb(f"act{b}", [P, CHUNK]) for b in range(3)]
        ah = sb("ah", [P, NH, USED], F32R)
        al = sb("al", [P, NH, USED], F32R)
        y_part = pair("y_part", [P, C])
        target = [sb(f"target{b}", [P, SLOT_TILES], U32) for b in range(2)]
        y = sb("y", [P, SLOT_TILES, C])

        x_first = sem("x_first"); x_rest = sem("x_rest")
        cst_in = sem("cst_in"); conv_in = sem("conv_in"); gate_in = sem("gate_in")
        w_in = [sem(f"w_in{b}") for b in range(2)]
        rows_in = [[sem(f"rows_in{b}_{go}") for go in range(2)] for b in range(2)]
        fills = sem("fills"); before_ready = sem("before_ready"); passed = sem("passed"); v_step = sem("v_step")
        var_a = sem("var_a"); sqrt_a = sem("sqrt_a"); q_ready = sem("q_ready"); f_ready = sem("f_ready")
        fc_copied = sem("fc_copied"); f_turned = sem("f_turned"); ft_ready = sem("ft_ready")
        gram_done = sem("gram_done"); gram_sb = sem("gram_sb")
        gram_out = [[sem(f"gram_out{h}_{b}") for b in range(2)] for h in range(2)]
        near_in = [sem(f"near_in{b}") for b in range(2)]
        corr_ready = sem("corr_ready"); c_turned = sem("c_turned"); ct_ready = sem("ct_ready")
        conv_done = sem("conv_done"); x1_ready = sem("x1_ready"); x1_out = sem("x1_out")
        var_b = sem("var_b"); sqrt_b = sem("sqrt_b"); tn_ready = sem("tn_ready")
        t_turned = sem("t_turned"); tt_ready = sem("tt_ready"); logits_done = sem("logits_done")
        choice_ready = sem("choice_ready"); place_done = sem("place_done"); tn_half = sem("tn_half"); seen_ready = sem("seen_ready"); shift_ready = sem("shift_ready")
        slot_ready = sem("slot_ready"); filled = sem("filled"); table_out = [sem(f"table_out{k}") for k in range(TOPK)]
        w_hi = sem("w_hi"); w_lo = sem("w_lo"); rows_turned = sem("rows_turned")
        x_hi = sem("x_hi"); x_lo = sem("x_lo"); h_done = sem("h_done")
        sil_ready = sem("sil_ready"); act_ready = sem("act_ready")
        a_hi = sem("a_hi"); a_lo = sem("a_lo")
        w_lo_first = sem("w_lo_first"); arg_ready = sem("arg_ready"); th_ready = sem("th_ready"); wt_ready = sem("wt_ready")
        y_done = sem("y_done"); y_half = sem("y_half"); y_ready = sem("y_ready"); added = sem("added")

        block = ctx.enter_context(nc.Block())

        SCATTERS = 16 * TILES
        W_LOADS = 16 * 4
        HT = NH * 2

        def pieces(b):
            r2, w2 = raw_2[b][:, :].rearrange("p (k n) -> p k n", k=NH), w_2[b]
            halves = [slice(0, H), slice(H, 2 * H)]
            return ([(raw_b[b][:, h], hi_b[b][:, h], lo_b[b][:, h]) for h in halves]
                    + [(raw_a[b][:, h], hi_a[b][:, h], lo_a[b][:, h]) for h in halves]
                    + [(r2[:, k, :], w2[:, k, 0, :], w2[:, k, 1, :]) for k in (slice(0, NH // 2), slice(NH // 2, NH))])

        PIECES = 6
        BLOCKS = [(c, j) for c in range(2) for j in range(NH)]
        REST_B = 2 * P

        def go_cut(go, first):
            if go == 0:
                return 0, FRONT_TILES, 0, CHUNK if first else FRONT_TILES * P, bank[7], 0
            if first:
                return FRONT_TILES - 1, SLOT_TILES, CHUNK, USED, bank[7], 0
            return FRONT_TILES, SLOT_TILES, FRONT_TILES * P, USED, bank[6], REST_B

        Y_BANK = [4, 5, 2, 3, 4]

        def alone(eng):
            eng.sem_inc(passed, 1)

        def experts(eng, run):
            run(0, 0, 0, True, False)
            with eng.Fori(0, (E - 2) // 2) as j:
                run(j * 2 + 1, j, 1, False, False)
                run(j * 2 + 2, j + 1, 0, False, False)
            run(E - 1, (E - 1) // 2, (E - 1) % 2, False, True)

        @block.sync
        def _(sp):
            xv = x.rearrange("(t p) c -> p t c", p=P)
            ov = out[0:TOKENS, :].rearrange("(t p) c -> p t c", p=P)
            sp.dma_start(xt[:, 0:TILES, :], xv[:, 0:TILES, :]).then_inc(x_first, 16)
            sp.dma_start(cst[:, :], consts).then_inc(cst_in, 16)
            sp.dma_start(xt[:, TILES:, :], xv[:, TILES:, :]).then_inc(x_rest, 16)
            sp.dma_start(conv_a[:, :], conv_wt[0:P, :]).then_inc(conv_in, 16)
            sp.dma_start(conv_b[:, :], conv_wt[P:, :]).then_inc(conv_in, 16)
            sp.dma_start(wg_a[:, :], wg[0:P, :]).then_inc(gate_in, 16)
            sp.dma_start(wg_b[:, :], wg[P:, :]).then_inc(gate_in, 16)

            def load_weights(e, b):
                w1e = w1[bass.ds(e, 1), :, :].rearrange("e k n -> (e k) n")
                w2e = w2[bass.ds(e, 1), :, :].rearrange("e (k p) n -> (e p) k n", p=P)
                sp.dma_start(raw_b[b][0:CB, :], w1e[P:C, :]).then_inc(w_in[b], 16)
                sp.dma_start(raw_b[b][CB:P, :], w1e[P:C, :]).then_inc(w_in[b], 16)
                sp.dma_start(raw_a[b][:, :], w1e[0:P, :]).then_inc(w_in[b], 16)
                sp.dma_start(raw_2[b][:, :].rearrange("p (k n) -> p k n", k=NH), w2e).then_inc(w_in[b], 16)

            def load_rows(e, b, first=False):
                whole = FRONT_TILES - 1
                for k in range(TOPK):
                    if first:
                        sp.wait_ge(table_out[k], SCATTERS * GROUPS)
                    tk = table[k][bass.ds(e * LIST, LIST), :]
                    if k == 0:
                        parts = [(rows[b][:, 0:whole, :], tk[0:whole * P, :]),
                                 (rows[b][0:EDGE, whole:whole + 1, :], tk[whole * P:CHUNK, :])]
                    else:
                        parts = [(rows[b][EDGE:P, whole:whole + 1, :], tk[0:P - EDGE, :]),
                                 (rows[b][:, whole + 1:, :], tk[P - EDGE:P - EDGE + (SLOT_TILES - FRONT_TILES) * P, :])]
                    for to, of in parts:
                        tiles = of.rearrange("(t p) r -> p t r", p=to.shape[0])
                        sp.dma_start(to[:, :, 0:C], tiles[:, :, 0:C]).then_inc(rows_in[b][k], 16)
                        sp.dma_start(to[:, :, C:], tiles[:, :, P:]).then_inc(rows_in[b][k], 16)

            def gram_round(g):
                b, turn = g % 2, g // 2
                for h in range(2):
                    sp.wait_ge(gram_sb, 2 * g + h + 1)
                    sp.dma_start(gram_dram[g, 2 * h:2 * h + 2, 0:P * WIN].rearrange("t (p w) -> p t w", w=WIN),
                                 gram[b][:, 2 * h:2 * h + 2, :]).then_inc(gram_out[h][b], 16)
                if g >= 2:
                    sp.wait_ge(corr_ready, g - 1)
                for h in range(2):
                    sp.wait_ge(gram_out[h][b], 16 * (turn + 1))
                    sp.dma_start(near[b][:, 2 * h:2 * h + 2, :],
                                 gram_dram[g, 2 * h:2 * h + 2, :].rearrange("t (p s) -> p t s", s=SKEW)[:, :, 0:SPAN]
                                 ).then_inc(near_in[b], 16)

            def store_x1(g):
                sp.wait_ge(x1_ready, g + 1)
                tiles = slice(g * TILES, (g + 1) * TILES)
                sp.dma_start(ov[:, tiles, :], xt[:, tiles, :]).then_inc(x1_out, 16)

            AHEAD = 3
            for g in range(AHEAD):
                gram_round(g)
            load_weights(0, 0)
            for g in range(GROUPS):
                store_x1(g)
                if g + AHEAD < GROUPS:
                    gram_round(g + AHEAD)
            load_weights(1, 1)

            load_rows(0, 0, True)

            def expert(e, half, b, first, last):
                if last:
                    return
                if not first:
                    sp.wait_ge(h_done, HT * e - (HT - 1))
                    load_weights(e + 1, 1 - b)
                    sp.wait_ge(rows_turned, 2 * e)
                    sp.wait_ge(arg_ready, e)
                load_rows(e + 1, 1 - b)

            experts(sp, expert)
            sp.wait_ge(x1_out, 16 * GROUPS)
            sp.wait_ge(added, 16 * SLOT_TILES * E)

        @block.gpsimd
        def _(pool):
            G = nc.gpsimd
            G.memset(eps_c[:, :], 1e-6)
            G.memset(eps_t[:, :], 1e-5)
            for b in range(2):
                for ft in (ft_a, ft_b):
                    G.memset(ft[b][:, 0:REACH], 0.0)
                    G.memset(ft[b][:, REACH + GROUP:], 0.0)
            G.memset(ones[:, :], 1.0)
            G.memset(seen[:, 0, :], 0.0)
            G.memset(empty[:, :, 0:C], 0.0)
            G.memset(empty[:, :, C + 1], 0.0)
            G.memset(empty[:, :, C], NO_TOKEN).then_inc(fills, 1)

            def fill_table(k):
                pool.wait_ge(fills, 1)
                rows_of = table[k].rearrange("(p f t) r -> p f t r", p=P, f=FILLS)
                for n in range(FILLS):
                    pool.dma_start(rows_of[:, n, :, :], empty[:, :, :]).then_inc(filled, 16)

            def copy_f(g):
                pool.wait_ge(f_ready, g + 1)
                if g >= 2:
                    pool.wait_ge(c_turned, g - 1)
                G.tensor_copy(fc[g % 2][:, :, 0:CB], f[g % 2][:, :, P:C]).then_inc(fc_copied, 1)

            def scatter(g):
                pool.wait_ge(slot_ready, g + 1)
                if g == 0:
                    pool.wait_ge(filled, 16 * TOPK * FILLS)
                for k in range(TOPK):
                    for t in range(TILES):
                        n = t * TOPK + k
                        G.indirect_dma_start(
                            out=table[k], out_offset=bass.IndirectOffsetOnAxis(ap=slot[g][:, n:n + 1], axis=0),
                            in_=row[g][:, t, :], in_offset=None,
                            bounds_check=E * LIST - 1, oob_is_err=False).then_inc(table_out[k], 16)

            def split_lo(e, b):
                for n, (raw, hi, lo) in enumerate(pieces(b)):
                    pool.wait_ge(w_hi, PIECES * e + n + 1)
                    G.tensor_tensor(lo, raw, hi.bitcast(F32), ALU.subtract).then_inc(w_lo, 1)

            fill_table(0)
            copy_f(0)
            copy_f(1)
            copy_f(2)
            fill_table(1)
            copy_f(3)
            for g in range(GROUPS):
                scatter(g)

            def expert(e, half, b, first, last):
                if not last:
                    split_lo(e + 1, 1 - b)
                for t in range(SLOT_TILES):
                    m = min(P, USED - t * P)
                    pool.wait_ge(y_ready, SLOT_TILES * e + t + 1)
                    if t == 0 and first:
                        pool.wait_ge(x1_out, 16 * GROUPS)
                    if t == 0 and not first:
                        pool.wait_ge(added, 16 * SLOT_TILES * e)
                    alone(pool)
                    nc.gpsimd.indirect_dma_start(
                        out=out, out_offset=bass.IndirectOffsetOnAxis(
                            ap=target[b][0:m, t:t + 1], axis=0),
                        in_=y[0:m, t, :], in_offset=None, compute_op=ALU.add).then_inc(added, 16)

            experts(pool, expert)

        @block.scalar
        def _(s):
            def tiles(g):
                return slice(g * TILES, (g + 1) * TILES)

            def deviation(g):
                s.wait_ge(var_a, g + 1)
                nc.scalar.activation(sd_a[:, tiles(g)], mv_a[:, tiles(g), 1], ACT.Sqrt, bias=eps_c[:, :])
                nc.scalar.activation(len_a[:, tiles(g)], mv_a[:, tiles(g), 1], ACT.Sqrt,
                                     scale=float(C)).then_inc(sqrt_a, 1)

            def features(g):
                s.wait_ge(q_ready, g + 1)
                if g >= 2:
                    s.wait_ge(f_turned, g - 1)
                    s.wait_ge(fc_copied, g - 1)
                for t in range(TILES):
                    n = g * TILES + t
                    last = nc.scalar.activation(f[g % 2][:, t, :], xt[:, n, :], ACT.Identity,
                                                bias=shift_a[:, n:n + 1], scale=q_a[:, n:n + 1])
                last.then_inc(f_ready, 1)

            def take_features(g):
                s.wait_ge(f_turned, g + 1)
                if g >= 2:
                    s.wait_ge(conv_done, g - 1)
                nc.scalar.copy(ft_a[g % 2][:, REACH:REACH + GROUP], bank[0][:, :])
                nc.scalar.copy(ft_b[g % 2][:, REACH:REACH + GROUP], bank[1][0:CB, :]).then_inc(ft_ready, 1)

            def take_gram(g):
                for h in range(2):
                    if g >= 2:
                        s.wait_ge(gram_out[h][g % 2], 16 * (g // 2))
                    s.wait_ge(gram_done, 2 * g + h + 1)
                    nc.scalar.copy(gram[g % 2][:, 2 * h:2 * h + 2, :],
                                   bank[2 + h][:, :].rearrange("p (t w) -> p t w", t=2)[:, :, 0:WIN]).then_inc(gram_sb, 1)

            def take_corr(g):
                s.wait_ge(c_turned, g + 1)
                nc.scalar.copy(ct[:, :], bank[5][0:CB + NCORR + 1, :]).then_inc(ct_ready, 1)

            def deviation_b(g):
                s.wait_ge(var_b, g + 1)
                nc.scalar.activation(sd_b[:, tiles(g)], mv_b[:, tiles(g), 1], ACT.Sqrt,
                                     bias=eps_t[:, :]).then_inc(sqrt_b, 1)

            def normed(g):
                s.wait_ge(shift_ready, g + 1)
                for t in range(TILES // 2, TILES):
                    n = g * TILES + t
                    last = nc.scalar.activation(row[g][:, t, 0:C], xt[:, n, :], ACT.Identity,
                                                bias=shift_b[:, n:n + 1], scale=rstd_b[:, n:n + 1])
                last.then_inc(tn_half, 1)

            def take_tokens(g):
                s.wait_ge(t_turned, g + 1)
                nc.scalar.copy(tt_a[:, :], bank[7][:, :])
                nc.scalar.copy(tt_b[:, :], bank[4][0:CB, :]).then_inc(tt_ready, 1)

            def split_hi(half, b, which):
                raw, hi, _ = pieces(b)[which]
                if which == 0:
                    s.wait_ge(w_in[b], W_LOADS * (half + 1))
                nc.scalar.copy(hi, raw).then_inc(w_hi, 1)

            s.wait_ge(fills, 1)
            nc.scalar.activation(warm[:, :], eps_t[:, :], ACT.Sqrt)
            deviation(0)
            features(0)
            deviation(1)
            take_features(0)
            features(1)
            take_gram(0)
            deviation(2)
            take_features(1)
            features(2)
            take_gram(1)
            take_corr(0)
            deviation(3)
            take_features(2)
            features(3)
            for g in range(GROUPS):
                if 1 <= g < GROUPS - 1:
                    take_corr(g + 1)
                deviation_b(g)
                normed(g)
                if g == 0:
                    take_gram(2)
                    take_corr(1)
                take_tokens(g)
                if g == 0:
                    take_features(3)
                    take_gram(3)
                else:
                    split_hi(0, 0, 2 * g - 2)
                    split_hi(0, 0, 2 * g - 1)
            nc.scalar.activation(warm[:, :], eps_t[:, :], ACT.Silu)

            def slots_hi(e, go, first=False):
                s.wait_ge(rows_turned, 2 * e + go + 1)
                tile, _, a, z, bank_b, off_b = go_cut(go, first)
                at = a - tile * P
                nc.scalar.copy(xh_a[:, a:z], bank[6][:, at:at + z - a]).then_inc(x_hi, 1)
                nc.scalar.copy(x_b[:, a:z], bank_b[:, off_b + at:off_b + at + z - a]).then_inc(x_hi, 1)

            slots_hi(0, 0, True)

            def expert(e, half, b, first, last):
                def hidden_hi(n):
                    c, j = BLOCKS[n]
                    lo, hi = CHUNKS[c]
                    s.wait_ge(act_ready, HT * e + n + 1)
                    nc.scalar.copy(ah[:, j, lo:hi], act[n % 3][:, 0:hi - lo]).then_inc(a_hi, 1)

                for n, (c, j) in enumerate(BLOCKS):
                    lo, hi = CHUNKS[c]
                    s.wait_ge(h_done, HT * e + n + 1)
                    if n >= 2 or not first:
                        s.wait_ge(act_ready, HT * e + n - 1)
                    nc.scalar.activation(sil[n % 2][:, 0:hi - lo], bank[2 * (n % 2) + 1][:, 0:hi - lo],
                                         ACT.Silu).then_inc(sil_ready, 1)
                    if n >= 1:
                        hidden_hi(n - 1)
                    if first and n == 2:
                        slots_hi(0, 1, True)
                    if n == 3:
                        s.wait_ge(arg_ready, e + 1)
                        nc.scalar.activation(th[:, :], arg[:, :], ACT.Tanh, scale=0.5).then_inc(th_ready, 1)
                    if n < PIECES and not last:
                        if n == 0 and not first:
                            s.wait_ge(y_done, SLOT_TILES * e)
                        split_hi(half if b == 0 else half + 1, 1 - b, n)
                hidden_hi(HT - 1)

                def half_y(t):
                    s.wait_ge(y_done, SLOT_TILES * e + t + 1)
                    if t >= 2 or not first:
                        s.wait_ge(y_ready, SLOT_TILES * e + t - 1)
                    m = min(P, USED - t * P)
                    nc.scalar.activation(y_part[t % 2][0:m, :], bank[Y_BANK[t]][0:m, C:2 * C], ACT.Copy,
                                         scale=wt[b][0:m, t:t + 1]).then_inc(y_half, 1)

                s.wait_ge(wt_ready, e + 1)
                if not last:
                    slots_hi(e + 1, 0)
                half_y(0)
                half_y(1)
                if not last:
                    slots_hi(e + 1, 1)
                for t in range(2, SLOT_TILES):
                    half_y(t)

            experts(s, expert)

        @block.vector
        def _(v):
            V = nc.vector
            step = Count(0)

            def tiles(g):
                return slice(g * TILES, (g + 1) * TILES)

            def then(ins):
                ins.then_inc(v_step, step.up())
                v.wait_ge(v_step, step.now)

            def stats(g):
                v.wait_ge(x_first if g == 0 else x_rest, 16)
                for t in range(g * TILES, (g + 1) * TILES):
                    last = V.bn_stats(stat_a[:, t, :], xt[:, t, :])
                then(last)
                for t in range(g * TILES, (g + 1) * TILES):
                    last = V.bn_aggr(mv_a[:, t, :], stat_a[:, t, :])
                last.then_inc(var_a, 1)

            def scales(g):
                n = tiles(g)
                v.wait_ge(sqrt_a, g + 1)
                then(V.reciprocal(rstd_a[:, n], sd_a[:, n]))
                then(V.tensor_tensor(nrm_a[:, n], len_a[:, n], rstd_a[:, n], ALU.mult))
                then(V.tensor_scalar(norm[:, n], nrm_a[:, n], 1e-12, None, ALU.max))
                then(V.reciprocal(inv_norm[:, n], norm[:, n]))
                then(V.tensor_tensor(q_a[:, n], rstd_a[:, n], inv_norm[:, n], ALU.mult))
                V.scalar_tensor_tensor(out=shift_a[:, n], in0=mv_a[:, n, 0], scalar=-1.0, in1=q_a[:, n],
                                       op0=ALU.mult, op1=ALU.mult).then_inc(q_ready, 1)

            def correlations(g):
                b = g % 2
                v.wait_ge(near_in[b], 32 * (g // 2 + 1))
                for n, (start, pitch) in enumerate([(0, SIDE + 1), (PAD, SIDE),
                                                    (2 * PAD, SIDE - 1), (PAD * SIDE, 1)]):
                    last = V.tensor_tensor(picked[:, :, n * K:(n + 1) * K],
                                           near[b][:, :, start:start + (K - 1) * pitch + 1:pitch],
                                           mask[:, :, n * K:(n + 1) * K], ALU.mult)
                if g >= 2:
                    v.wait_ge(c_turned, g - 1)
                V.tensor_copy(fc[b][:, :, CB + NCORR:], inv_norm[:, tiles(g)].unsqueeze(2))
                then(last)
                V.tensor_tensor(fc[b][:, :, CB:CB + NCORR], picked[:, :, :],
                                inv_norm[:, tiles(g)].unsqueeze(2).broadcast_to([P, TILES, NCORR]),
                                ALU.mult).then_inc(corr_ready, 1)

            def residual(g):
                b = g % 2
                v.wait_ge(conv_done, g + 1)
                for t in range(TILES):
                    n = g * TILES + t
                    last = V.scalar_tensor_tensor(out=xt[:, n, :], in0=bank[5 + t // 2][:, 256 * (t % 2):256 * (t % 2) + C],
                                                  scalar=norm[:, n:n + 1], in1=xt[:, n, :],
                                                  op0=ALU.mult, op1=ALU.add)
                last.then_inc(x1_ready, 1)
                v.wait_ge(x1_ready, g + 1)
                for n in range(g * TILES, (g + 1) * TILES):
                    last = V.bn_stats(stat_b[:, n, :], xt[:, n, :])
                then(last)
                for n in range(g * TILES, (g + 1) * TILES):
                    last = V.bn_aggr(mv_b[:, n, :], stat_b[:, n, :])
                last.then_inc(var_b, 1)

            def normed(g):
                v.wait_ge(sqrt_b, g + 1)
                then(V.reciprocal(rstd_b[:, tiles(g)], sd_b[:, tiles(g)]))
                V.scalar_tensor_tensor(out=shift_b[:, tiles(g)], in0=mv_b[:, tiles(g), 0], scalar=-1.0,
                                       in1=rstd_b[:, tiles(g)], op0=ALU.mult, op1=ALU.mult).then_inc(shift_ready, 1)
                V.tensor_copy(row[g][:, :, C], cst[:, C_TOK + g * TILES:C_TOK + (g + 1) * TILES])
                for t in range(TILES // 2):
                    n = g * TILES + t
                    last = V.tensor_scalar(row[g][:, t, 0:C], xt[:, n, :], mv_b[:, n, 0:1], rstd_b[:, n:n + 1],
                                           ALU.subtract, ALU.mult)
                last.then_inc(tn_ready, 1)

            def choose(g):
                v.wait_ge(logits_done, g + 1)
                for t in range(TILES):
                    last = V.max(top[:, t, :], bank[7][:, t * E:(t + 1) * E])
                then(last)
                for t in range(TILES):
                    last = V.max_index(top_e[:, t, :], top[:, t, :], bank[7][:, t * E:(t + 1) * E])
                then(last)
                then(V.tensor_copy(pick[:, :, :], top_e[:, :, 0:TOPK]))
                V.tensor_tensor(onehot[:, :, :, :].rearrange("p t k e -> p (t k) e"),
                                iota.unsqueeze(1).broadcast_to([P, TILES * TOPK, E]),
                                pick[:, :, :].rearrange("p t k -> p (t k)").unsqueeze(2).broadcast_to([P, TILES * TOPK, E]),
                                ALU.is_equal).then_inc(choice_ready, 1)
                V.tensor_tensor(row[g][:, :, C + 1], top[:, :, 1], top[:, :, 0], ALU.subtract)
                if g + 1 < GROUPS:
                    v.wait_ge(choice_ready, g + 1)
                    then(V.tensor_reduce(chosen[:, :], onehot[:, :, :, :].rearrange("p t k e -> p (k e) t"),
                                         AX_X, ALU.add))
                    V.tensor_tensor(seen[:, g + 1, :], seen[:, g, :], chosen[:, :], ALU.add).then_inc(seen_ready, 1)

            def find_slots(g):
                v.wait_ge(place_done, g + 1)
                then(V.tensor_tensor(place_e[:, :, :],
                                     bank[7][:, 2 * P:2 * P + TILES * TOPK * E].rearrange("p (n e) -> p n e", e=E),
                                     onehot[:, :, :, :].rearrange("p t k e -> p (t k) e"), ALU.mult))
                then(V.tensor_reduce(place[:, :], place_e[:, :, :], AX_X, ALU.add))
                V.tensor_scalar(miss[:, :], place[:, :], float(CAP), MISS, ALU.is_ge, ALU.mult)
                then(V.scalar_tensor_tensor(out=slot_f[:, :], in0=pick[:, :, :].rearrange("p t k -> p (t k)"),
                                            scalar=float(LIST), in1=place[:, :], op0=ALU.mult, op1=ALU.add))
                V.tensor_tensor(slot[g][:, :], slot_f[:, :], miss[:, :], ALU.add).then_inc(slot_ready, 1)

            stats(0)
            scales(0)
            v.wait_ge(fills, 1)
            v.wait_ge(cst_in, 16)
            V.tensor_copy(before[:, :], cst[:, C_UPPER:C_UPPER + P]).then_inc(before_ready, 1)
            for g in (1, 2):
                stats(g)
                scales(g)
            correlations(0)
            stats(3)
            scales(3)
            for g in range(GROUPS):
                residual(g)
                if g + 1 < GROUPS:
                    correlations(g + 1)
                if g >= 1:
                    choose(g - 1)
                    find_slots(g - 1)
                normed(g)
            choose(GROUPS - 1)
            find_slots(GROUPS - 1)

            def slots_lo(e, go, first=False):
                tile, _, a, z, bank_b, off_b = go_cut(go, first)
                at = a - tile * P
                v.wait_ge(x_hi, 4 * e + 2 * go + 1 + go)
                V.tensor_tensor(xl_a[:, a:z], bank[6][:, at:at + z - a], xh_a[:, a:z].bitcast(F32),
                                ALU.subtract).then_inc(x_lo, 1)
                v.wait_ge(x_hi, 4 * e + 2 * go + 2)
                V.tensor_tensor(x_b[CB:P, a:z], bank_b[CB:P, off_b + at:off_b + at + z - a], x_b[CB:P, a:z].bitcast(F32),
                                ALU.subtract).then_inc(x_lo, 1)

            for n, (raw, hi, lo) in enumerate(pieces(0)):
                v.wait_ge(w_hi, n + 1)
                V.tensor_tensor(lo, raw, hi.bitcast(F32), ALU.subtract).then_inc(w_lo_first, 1)
            slots_lo(0, 0, True)

            def expert(e, half, b, first, last):
                def hidden_lo(n):
                    c, j = BLOCKS[n]
                    lo, hi = CHUNKS[c]
                    v.wait_ge(a_hi, HT * e + n + 1)
                    V.tensor_tensor(al[:, j, lo:hi], act[n % 3][:, 0:hi - lo], ah[:, j, lo:hi].bitcast(F32),
                                    ALU.subtract).then_inc(a_lo, 1)

                for n, (c, j) in enumerate(BLOCKS):
                    lo, hi = CHUNKS[c]
                    if n >= 3 or not first:
                        v.wait_ge(a_lo, HT * e + n - 2)
                    v.wait_ge(sil_ready, HT * e + n + 1)
                    V.tensor_tensor(act[n % 3][:, 0:hi - lo], bank[2 * (n % 2)][:, 0:hi - lo],
                                    sil[n % 2][:, 0:hi - lo], ALU.mult).then_inc(act_ready, 1)
                    if n >= 1:
                        hidden_lo(n - 1)
                    if first and n == 2:
                        slots_lo(0, 1, True)
                    if n == 2:
                        for go in range(2):
                            v.wait_ge(rows_in[b][go], 64 * (half + 1))
                        V.tensor_tensor(target[b][:, :], rows[b][:, :, C + CB], spare, ALU.min)
                        V.tensor_tensor(arg[:, :], rows[b][:, :, C + CB + 1], sign, ALU.mult).then_inc(arg_ready, 1)
                    if n == 4:
                        v.wait_ge(th_ready, e + 1)
                        V.tensor_scalar(wt[b][:, :], th[:, :], 0.5, 0.5, ALU.mult, ALU.add).then_inc(wt_ready, 1)
                hidden_lo(HT - 1)

                v.wait_ge(wt_ready, e + 1)

                def take_y(t):
                    v.wait_ge(y_done, SLOT_TILES * e + t + 1)
                    m = min(P, USED - t * P)
                    v.wait_ge(y_half, SLOT_TILES * e + t + 1)
                    V.scalar_tensor_tensor(out=y[0:m, t, :], in0=bank[Y_BANK[t]][0:m, 0:C],
                                           scalar=wt[b][0:m, t:t + 1], in1=y_part[t % 2][0:m, :],
                                           op0=ALU.mult, op1=ALU.add).then_inc(y_ready, 1)

                if not first:
                    v.wait_ge(added, 16 * SLOT_TILES * e)
                if last:
                    for t in range(SLOT_TILES):
                        take_y(t)
                    return
                slots_lo(e + 1, 0)
                take_y(0)
                take_y(1)
                slots_lo(e + 1, 1)
                for t in range(2, SLOT_TILES):
                    take_y(t)

            experts(v, expert)

        @block.tensor
        def _(pe):
            T = nc.tensor

            BUSY_START, BUSY_FIRST, BUSY, BUSY_BEFORE, BUSY_END = 14, 4, 6, 8, 46

            def keep_busy(n, idle):
                for _ in range(n):
                    T.matmul(idle[:, :], ones[:, :], ones[:, :].unsqueeze(1).broadcast_to([P, 4, P]),
                             start=True, stop=True)

            def turn_f(g):
                if g >= 1:
                    pe.wait_ge(ft_ready, g)
                pe.wait_ge(f_ready, g + 1)
                for t in range(TILES):
                    T.transpose(bank[0][:, t * P:(t + 1) * P], f[g % 2][:, t, 0:P], ident)
                    last = T.transpose(bank[1][0:CB, t * P:(t + 1) * P], f[g % 2][:, t, P:C], ident)
                last.then_inc(f_turned, 1)

            def grams(g):
                pe.wait_ge(ft_ready, g + 1)
                if g >= 1:
                    pe.wait_ge(gram_sb, 2 * g)
                fa, fb = ft_a[g % 2], ft_b[g % 2]
                for t in range(TILES):
                    o = bank[2 + t // 2][:, 256 * (t % 2):256 * (t % 2) + WIN]
                    own = slice(REACH + t * P, REACH + (t + 1) * P)
                    win = slice(t * P, t * P + WIN)
                    T.matmul(o, fa[:, own], fa[:, win], start=True, stop=False)
                    last = T.matmul(o, fb[:, own], fb[:, win], start=False, stop=True)
                    if t % 2:
                        last.then_inc(gram_done, 1)

            def turn_corr(g):
                if g >= 1:
                    pe.wait_ge(x1_ready, g)
                pe.wait_ge(fc_copied, g + 1)
                pe.wait_ge(corr_ready, g + 1)
                for t in range(TILES):
                    last = T.transpose(bank[5][0:CB + NCORR + 1, t * P:(t + 1) * P], fc[g % 2][:, t, :], ident)
                last.then_inc(c_turned, 1)

            def conv(g):
                if g == 0:
                    pe.wait_ge(conv_in, 32)
                pe.wait_ge(ct_ready, g + 1)
                for t in range(TILES):
                    o = bank[5 + t // 2][:, 256 * (t % 2):256 * (t % 2) + C]
                    T.matmul(o, ft_a[g % 2][:, REACH + t * P:REACH + (t + 1) * P], conv_a[:, :], start=True, stop=False)
                    last = T.matmul(o, ct[:, t * P:(t + 1) * P], conv_b[:, :], start=False, stop=True)
                last.then_inc(conv_done, 1)

            def turn_tokens(g):
                pe.wait_ge(tn_ready, g + 1)
                pe.wait_ge(tn_half, g + 1)
                if g >= 1:
                    pe.wait_ge(slot_ready, g)
                for t in range(TILES):
                    T.transpose(bank[7][:, t * P:(t + 1) * P], row[g][:, t, 0:P], ident)
                    last = T.transpose(bank[4][0:CB, t * P:(t + 1) * P], row[g][:, t, P:C], ident)
                last.then_inc(t_turned, 1)

            def logits(g):
                if g == 0:
                    pe.wait_ge(gate_in, 32)
                pe.wait_ge(tt_ready, g + 1)
                for t in range(TILES):
                    o = bank[7][:, t * E:(t + 1) * E]
                    T.matmul(o, tt_a[:, t * P:(t + 1) * P], wg_a[:, :], start=True, stop=False)
                    last = T.matmul(o, tt_b[:, t * P:(t + 1) * P], wg_b[:, :], start=False, stop=True)
                last.then_inc(logits_done, 1)

            def places(g):
                if g == 0:
                    pe.wait_ge(before_ready, 1)
                pe.wait_ge(choice_ready, g + 1)
                o = bank[7][:, 2 * P:2 * P + TILES * TOPK * E]
                picks = onehot[:, :, :, :].rearrange("p t k e -> p (t k e)")
                T.matmul(o, before[:, :], picks, start=True, stop=False)
                for d in range(1, TILES):
                    n = d * TOPK * E
                    T.matmul(o[:, n:], ones[:, :], picks[:, 0:TILES * TOPK * E - n], start=False, stop=False,
                             skip_group_check=True)
                if g >= 1:
                    pe.wait_ge(seen_ready, g)
                T.matmul(o, ones[:, :], seen[:, g, :].unsqueeze(1).broadcast_to([P, TILES, TOPK * E]),
                         start=False, stop=True).then_inc(place_done, 1)

            pe.wait_ge(fills, 1)
            keep_busy(BUSY_START, bank[0])
            pe.wait_ge(cst_in, 16)
            for g in (0, 1):
                turn_f(g)
                grams(g)
            turn_f(2)
            keep_busy(BUSY_FIRST, bank[7])
            turn_corr(0)
            conv(0)
            grams(2)
            for g in range(GROUPS):
                if g + 1 < GROUPS:
                    turn_corr(g + 1)
                if g == 0:
                    turn_tokens(0)
                if g >= 1:
                    places(g - 1)
                if g + 1 < GROUPS:
                    conv(g + 1)
                if g == GROUPS - 1:
                    keep_busy(BUSY_BEFORE, bank[0])
                if g >= 1:
                    turn_tokens(g)
                    keep_busy(BUSY, bank[0])
                else:
                    turn_f(3)
                logits(g)
                if g == 0:
                    grams(3)
            keep_busy(BUSY, bank[0])
            places(GROUPS - 1)
            keep_busy(BUSY_END, bank[0])

            def turn_rows(e, half, b, go, first=False):
                start, end, _, _, bank_b, off_b = go_cut(go, first)
                pe.wait_ge(rows_in[b][go], 64 * (half + 1))
                if go == 0 and not first:
                    pe.wait_ge(rows_in[b][1], 64 * (half + 1))
                if go == 1:
                    pe.wait_ge(x_lo, 4 * e + (2 if first else 1))
                for t in range(start, end):
                    at = (t - start) * P
                    m = EDGE if first and go == 0 and t == end - 1 else P
                    T.transpose(bank[6][:, at:at + m], rows[b][0:m, t, 0:P], ident[0:m, 0:m])
                    last = T.transpose(bank_b[:, off_b + at:off_b + at + m], rows[b][0:m, t, P:P + 2 * CB], ident[0:m, 0:m])
                last.then_inc(rows_turned, 1)

            turn_rows(0, 0, 0, 0, True)

            def expert(e, half, b, first, last):
                pe.wait_ge(w_hi, PIECES * (e + 1))
                if first:
                    pe.wait_ge(w_lo_first, PIECES)
                else:
                    pe.wait_ge(w_lo, PIECES * e)
                for n, (c, j) in enumerate(BLOCKS):
                    lo, hi = CHUNKS[c]
                    if first and n == 2:
                        turn_rows(0, 0, 0, 1, True)
                    if n >= 2 or not first:
                        pe.wait_ge(act_ready, HT * e + n - 1)
                    if n == 1 and not first:
                        pe.wait_ge(y_ready, SLOT_TILES * e - 1)
                    for half_h in range(2):
                        o = bank[2 * (n % 2) + half_h][:, 0:hi - lo]
                        cols = slice((half_h * NH + j) * P, (half_h * NH + j + 1) * P)
                        if j == 0 and half_h == 0:
                            pe.wait_ge(x_hi, 4 * e + 2 * c + 1)
                        T.matmul(o, hi_a[b][:, cols], xh_a[:, lo:hi], start=True, stop=False)
                        T.matmul(o, lo_a[b][:, cols], xh_a[:, lo:hi], start=False, stop=False)
                        if j == 0 and half_h == 0:
                            pe.wait_ge(x_lo, 4 * e + 2 * c + 1)
                        T.matmul(o, hi_a[b][:, cols], xl_a[:, lo:hi], start=False, stop=False)
                        if j == 0 and half_h == 0:
                            pe.wait_ge(x_lo, 4 * e + 2 * c + 2)
                        T.matmul(o, hi_b[b][:, cols], x_b[:, lo:hi], start=False, stop=False)
                        mm = T.matmul(o, lo_b[b][:, cols], x_b[:, lo:hi], start=False, stop=True)
                    mm.then_inc(h_done, 1)

                def out_tile(t):
                    m = min(P, USED - t * P)
                    pe.wait_ge(a_lo, HT * e + (NH if (t + 1) * P <= CHUNK else HT))
                    if t == 0 and not first:
                        pe.wait_ge(y_ready, SLOT_TILES * e)
                    if t == 4:
                        pe.wait_ge(y_ready, SLOT_TILES * e + 1)
                    acc = bank[Y_BANK[t]][0:m, 0:2 * C]
                    cols = slice(t * P, t * P + m)
                    for j in range(NH):
                        T.matmul(acc, ah[:, j, cols], w_2[b][:, j, :, :].rearrange("p h n -> p (h n)"),
                                 start=(j == 0), stop=(j == NH - 1))
                        mm = T.matmul(acc[:, 0:C], al[:, j, cols], w_2[b][:, j, 0, :],
                                      start=False, stop=(j == NH - 1), skip_group_check=True)
                    mm.then_inc(y_done, 1)

                if not last:
                    nxt = half if b == 0 else half + 1
                    turn_rows(e + 1, nxt, 1 - b, 0)
                out_tile(0)
                out_tile(1)
                if not last:
                    turn_rows(e + 1, nxt, 1 - b, 1)
                for t in range(2, SLOT_TILES):
                    out_tile(t)

            experts(pe, expert)


def kernel(x, L0_conv_conv_w, L0_conv_conv_b, L0_ffn_Wg, L0_ffn_W1, L0_ffn_W2):
    import concourse.bacc as bacc
    from concourse.bass_utils import run_bass_kernel_spmd

    arrays = {
        "x_tokens": np.ascontiguousarray(np.asarray(x).reshape(IMAGES, C, PIXELS).transpose(0, 2, 1).reshape(TOKENS, C)),
        "conv_wt": np.concatenate([np.asarray(L0_conv_conv_w).T, np.asarray(L0_conv_conv_b)[None, :]]),
        "wg": np.ascontiguousarray(L0_ffn_Wg),
        "w1": np.ascontiguousarray(L0_ffn_W1),
        "w2": np.ascontiguousarray(L0_ffn_W2),
        "consts": constants(),
    }
    nc = bacc.Bacc("TRN2", target_bir_lowering=False, num_devices=1)
    args = [nc.dram_tensor(n, a.shape, mybir.dt.from_np(a.dtype), kind="ExternalInput").ap() for n, a in arrays.items()]
    out = nc.dram_tensor("out", (TOKENS + SLOTS, C), F32, kind="ExternalOutput").ap()
    metaformer_kernel(nc, *args, out)
    r = run_bass_kernel_spmd(nc, [arrays], core_ids=[0])
    got = r.results[0]["out"][0:TOKENS]
    return np.ascontiguousarray(got.reshape(IMAGES, PIXELS, C).transpose(0, 2, 1).reshape(IMAGES, C, SIDE, SIDE))
```
